# Optimizing a Trainium2 kernel written in Bass

```python
import numpy as np
import jax
import jax.numpy as jnp

def _softmax(x, axis=-1):
    return jax.nn.softmax(x, axis=axis)

def _gelu(x):
    return jax.nn.gelu(x, approximate=True)

def _silu(x):
    return jax.nn.silu(x)

def _sigmoid(x):
    return jax.nn.sigmoid(x)

def _layernorm(x, axis=-1, eps=1e-05):
    m = jnp.mean(x, axis=axis, keepdims=True)
    v = jnp.var(x, axis=axis, keepdims=True)
    return (x - m) / jnp.sqrt(v + eps)

def _scatter_add(tgt, idx, src, axis=0):
    return tgt.at[idx].add(src)

def _segment_sum(src, seg, n):
    return jax.ops.segment_sum(src, seg, n)
kernel_name = 'mk_gnn_resnorm_d1_gnn_r32_1c1727'

def setup_inputs(seed: int=0):
    np.random.seed(seed)
    _w = jnp.asarray

    def _rec_inputs():
        import jax
        import jax.numpy as jnp
        _gk = jax.random.key(seed)
        x = -0.001812 + 1 * jax.random.normal(jax.random.fold_in(_gk, 1), (3125, 32), jnp.float32)
        _s = jax.random.randint(jax.random.fold_in(_gk, 2), (25000,), 0, 3125, jnp.int32)
        _d = jax.random.randint(jax.random.fold_in(_gk, 3), (25000,), 0, 3125, jnp.int32)
        _loop = jnp.arange(3125, dtype=jnp.int32)
        src = jnp.concatenate([_s, _d, _loop])
        dst = jnp.concatenate([_d, _s, _loop])
        _o = jnp.argsort(dst, stable=True)
        src = src[_o]
        dst = dst[_o]
        edge_attr_10 = jax.random.uniform(jax.random.fold_in(_gk, 12), (53125, 10), jnp.float32, 0.0, 0.999998)
        edge_attr_3 = 0.00158508 + 0.999651 * jax.random.normal(jax.random.fold_in(_gk, 13), (53125, 3), jnp.float32)
        edge_weight = jax.random.uniform(jax.random.fold_in(_gk, 14), (53125,), jnp.float32, 0.0, 0.999997)
        return (x, src, dst, edge_attr_10, edge_attr_3, edge_weight)
    x, src, dst, edge_attr_10, edge_attr_3, edge_weight = _rec_inputs()

    def _L0_gnn_setup():
        import jax, jax.numpy as jnp
        import numpy as np
        SQRT3 = 3.0 ** 0.5

        def _mlp(emb, w1, w2):
            h = jax.nn.relu(emb @ w1 / jnp.sqrt(jnp.float32(w1.shape[0])))
            return h @ w2 / jnp.sqrt(jnp.float32(w2.shape[0]))
        key = jax.random.key(seed)
        ks = jax.random.split(key, 10)
        N, E = (10000, 5000)
        x = jax.random.normal(ks[0], (N, 32), jnp.float32)
        edge_src = jax.random.randint(ks[1], (E,), 0, N)
        edge_dst = jax.random.randint(ks[2], (E,), 0, N)
        edge_vec = jax.random.normal(ks[3], (E, 3), jnp.float32)
        emb = jax.random.uniform(ks[4], (E, 10), jnp.float32)
        norm = jax.random.uniform(ks[5], (E,), jnp.float32)
        fc1_w1 = jax.random.normal(ks[6], (10, 16), jnp.float32)
        fc1_w2 = jax.random.normal(ks[7], (16, 512), jnp.float32)
        fc2_w1 = jax.random.normal(ks[8], (10, 16), jnp.float32)
        fc2_w2 = jax.random.normal(ks[9], (16, 384), jnp.float32)
        return dict(x=x, edge_src=edge_src, edge_dst=edge_dst, edge_vec=edge_vec, emb=emb, norm=norm, num_nodes=N, fc1_w1=fc1_w1, fc1_w2=fc1_w2, fc2_w1=fc2_w1, fc2_w2=fc2_w2)
    _L0_gnn_all = _L0_gnn_setup()
    _L0_gnn_in = {k: v for k, v in _L0_gnn_all.items() if k in ('fc1_w1', 'fc1_w2', 'fc2_w1', 'fc2_w2')}
    del _L0_gnn_all
    return {'x': x, 'src': src, 'dst': dst, 'edge_attr_10': edge_attr_10, 'edge_attr_3': edge_attr_3, 'edge_weight': edge_weight, 'L0_gnn_fc1_w1': _L0_gnn_in['fc1_w1'], 'L0_gnn_fc1_w2': _L0_gnn_in['fc1_w2'], 'L0_gnn_fc2_w1': _L0_gnn_in['fc2_w1'], 'L0_gnn_fc2_w2': _L0_gnn_in['fc2_w2']}

def reference(x, src, dst, edge_attr_10, edge_attr_3, edge_weight, L0_gnn_fc1_w1, L0_gnn_fc1_w2, L0_gnn_fc2_w1, L0_gnn_fc2_w2):
    import jax
    import jax.numpy as jnp

    def _L0_gnn_ref(x, edge_src, edge_dst, edge_vec, emb, norm, num_nodes, fc1_w1, fc1_w2, fc2_w1, fc2_w2):
        import jax, jax.numpy as jnp
        import numpy as np
        SQRT3 = 3.0 ** 0.5

        def _mlp(emb, w1, w2):
            h = jax.nn.relu(emb @ w1 / jnp.sqrt(jnp.float32(w1.shape[0])))
            return h @ w2 / jnp.sqrt(jnp.float32(w2.shape[0]))
        E = edge_vec.shape[0]
        r = edge_vec / jnp.linalg.norm(edge_vec, axis=1, keepdims=True)
        sh1 = SQRT3 * r
        xs, xd = (x[edge_src], x[edge_dst])
        s1 = jnp.concatenate([xs[:, :8], xd[:, :8]], axis=1)
        v1 = jnp.concatenate([xs[:, 8:].reshape(E, 8, 3), xd[:, 8:].reshape(E, 8, 3)], axis=1)
        w = _mlp(emb, fc1_w1, fc1_w2)
        Wss = w[:, 0:128].reshape(E, 16, 8)
        Wvv = w[:, 128:256].reshape(E, 16, 8)
        Wsv = w[:, 256:384].reshape(E, 16, 8)
        Wvs = w[:, 384:512].reshape(E, 16, 8)
        a1 = 1.0 / jnp.sqrt(32.0)
        vdot1 = jnp.einsum('euk,ek->eu', v1, sh1) / SQRT3
        s_t = a1 * (jnp.einsum('eu,euw->ew', s1, Wss) + jnp.einsum('eu,euw->ew', vdot1, Wvv))
        v_t = a1 * (jnp.einsum('eu,euw->ew', s1, Wsv)[:, :, None] * sh1[:, None, :] + jnp.einsum('euk,euw->ewk', v1, Wvs))
        w2 = _mlp(emb, fc2_w1, fc2_w2)
        Ass = w2[:, 0:64].reshape(E, 8, 8)
        Avv = w2[:, 64:128].reshape(E, 8, 8)
        Bss = w2[:, 128:192].reshape(E, 8, 8)
        Bvv = w2[:, 192:256].reshape(E, 8, 8)
        Csv = w2[:, 256:320].reshape(E, 8, 8)
        Cvs = w2[:, 320:384].reshape(E, 8, 8)
        a2 = 1.0 / jnp.sqrt(16.0)
        vdot2 = jnp.einsum('euk,ek->eu', v_t, sh1) / SQRT3
        scal = a2 * (jnp.einsum('eu,euw->ew', s_t, Ass) + jnp.einsum('eu,euw->ew', vdot2, Avv))
        gates = a2 * (jnp.einsum('eu,euw->ew', s_t, Bss) + jnp.einsum('eu,euw->ew', vdot2, Bvv))
        vecs = a2 * (jnp.einsum('eu,euw->ew', s_t, Csv)[:, :, None] * sh1[:, None, :] + jnp.einsum('euk,euw->ewk', v_t, Cvs))
        edge_out = jnp.concatenate([jnp.tanh(scal), (vecs * jnp.tanh(gates)[:, :, None]).reshape(E, 24)], axis=1)
        edge_out = edge_out * norm[:, None]
        return jax.ops.segment_sum(edge_out, edge_dst, num_segments=num_nodes)
    x = _layernorm(x + _L0_gnn_ref(x, src, dst, edge_attr_3, edge_attr_10, edge_weight, 3125, L0_gnn_fc1_w1, L0_gnn_fc1_w2, L0_gnn_fc2_w1, L0_gnn_fc2_w2), axis=-1)
    return x

_drawn_inputs = setup_inputs


def setup_inputs(seed=0):
    import zlib

    import numpy as np

    out = dict(_drawn_inputs(seed))
    spreads = {}
    factors = {}
    for name, (base, spread) in spreads.items():
        noise = np.random.default_rng([zlib.crc32(name.encode()), seed]).standard_normal(out[name].shape)
        drawn = base * np.exp(spread * noise) if base else spread * noise
        out[name] = jnp.asarray(drawn.astype(out[name].dtype))
    for name, factor in factors.items():
        out[name] = (out[name] * factor).astype(out[name].dtype)
    return out
```

```python
import math
from contextlib import ExitStack

import concourse.bass as bass
from concourse import mybir

F32 = mybir.dt.float32
BF16 = mybir.dt.bfloat16
I32 = mybir.dt.int32
ALU = mybir.AluOpType
ACT = mybir.ActivationFunctionType
AX = mybir.AxisListType

N = 3125
E = 53125
D = 32
P = 125
T = 5
BE = P * T
NB = E // BE
J = 16
W = 8
V1 = 16
V2 = 8
K1 = 6
K2 = 8
O1 = 5
O2 = 6
C1 = 4 * V1 * W
C2 = 6 * V2 * W
WIN = 64
HALF1 = 5
SLOTS = ((0, 0), (0, 1), (0, 2), (1, 0), (1, 1), (2, 0))
S = len(SLOTS)
NT = N // P
RING = 4
SQRT3 = math.sqrt(3.0)
EPS = 1e-5


class Block:

    def __init__(self, turn, c):
        self.turn, self.c = turn, c

    def __add__(self, d):
        return Block(self.turn, self.c + d)

    def times(self, k, plus=0):
        if isinstance(self.turn, int):
            return k * (RING * self.turn + self.c) + plus
        return self.turn * (RING * k) + (k * self.c + plus)

    def turns(self, k, plus=0):
        return self.turn * k + (k * (self.c // RING) + plus)

    def pairs(self, k, plus=0):
        return self.turn * (RING // 2 * k) + (k * (self.c // 2) + plus)

    @property
    def known(self):
        return self.c if isinstance(self.turn, int) else min(max(self.c, RING), NB - RING)

    @property
    def real(self):
        return 0 <= self.c < NB or not isinstance(self.turn, int)


def program(nc, x, src, dst, emb, vec, weight, w11, w12, w21, w22, out):
    ctx = ExitStack()
    with ctx:
        def sb(name, shape, dt=F32):
            return ctx.enter_context(nc.sbuf_tensor(name, shape, dt))

        def sem(name):
            return ctx.enter_context(nc.semaphore(name))

        ident = sb("ident", [128, 128])
        iota_i = sb("iota_i", [P, P], I32)
        iota = sb("iota", [P, P])
        ones = sb("ones", [P, 1])
        slot_mask = sb("slot_mask", [S * J, 4])
        w2f = sb("w2f", [S * J, C1 + C2])
        w2part = [sb(f"w2part{n}", [S * J, C1 + C2], BF16) for n in range(3)]
        w2s = sb("w2s", [S * J, C1 + C2], BF16)
        w1bd = sb("w1bd", [T * 10, T, 2, J])
        ident_h = sb("ident_h", [P, P], BF16)
        vec_b = sb("vec_b", [NB, BE, 3])
        dst_b = sb("dst_b", [NB, BE], I32)
        dstf_b = sb("dstf_b", [NB, BE])
        wgt_b = sb("wgt_b", [NB, BE])
        n2_b = sb("n2_b", [NB, BE])
        nrm_b = sb("nrm_b", [NB, BE])
        inv_b = sb("inv_b", [NB, BE])
        geo_b = sb("geo_b", [NB, BE, 5])
        ext = sb("ext", [NB, 4])
        misfits = sb("misfits", [1, 1], I32)
        bases = sb("bases", [1, NB], I32)
        geo_dram = nc.dram_tensor("geo_dram", (E, 5), F32, kind="Internal").ap()
        src_r = [sb(f"src{n}", [P, T], I32) for n in range(RING)]
        dst_r = [sb(f"dst{n}", [P, T], I32) for n in range(RING)]
        emb_r = [sb(f"emb{n}", [P, T * 10]) for n in range(RING)]
        geo_r = [sb(f"geo{n}", [P, T, 5]) for n in range(RING)]
        x_r = [sb(f"x{n}", [P, T, 2, D]) for n in range(RING)]
        h_r = [sb(f"h{n}", [P, T, 2, J]) for n in range(2)]
        hp_r = [sb(f"hp{n}", [P, 2, T, S, J], BF16) for n in range(2)]
        ht_r = [[sb(f"ht{k}_{n}", [S * J, T * P], BF16) for n in range(2)] for k in range(2)]
        f1_r = [sb(f"f1_{n}", [P, T, K1, V1]) for n in range(2)]
        f2_r = [sb(f"f2_{n}", [P, T, K2, V2]) for n in range(2)]
        embt_r = [sb(f"embt{n}", [T * 10, P]) for n in range(2)]
        p1_r = [sb(f"p1_{n}", [P, V1, T, K1, W]) for n in range(2)]
        p2_r = [sb(f"p2_{n}", [P, V2, T, K2, W]) for n in range(2)]
        th_r = [sb(f"th{n}", [P, T, 2, W]) for n in range(2)]
        eo_r = [sb(f"eo{n}", [P, T, D]) for n in range(2)]
        oh_r = [sb(f"oh{n}", [P, T, WIN]) for n in range(2)]
        far = sb("far", [P, T, WIN])
        tmp1 = sb("tmp1", [P, T, 3, V1])
        tmp2 = sb("tmp2", [P, T, 3, W])
        tmp3 = sb("tmp3", [P, T, 3, W])
        tmp4 = sb("tmp4", [P, T, 3, W])
        gate = sb("gate", [P, T, W])
        acc = sb("acc", [D, N + WIN])
        eo_all = sb("eo_all", [P, NB, T * D])
        eo_s = sb("eo_s", [P, T, D])
        dst_all = sb("dst_all", [P, NB, T], I32)
        dst_w = sb("dst_w", [P, T])
        oh_w = sb("oh_w", [P, T, P])
        xn = sb("xn", [P, NT, D])
        yn = sb("yn", [P, NT, D])
        st = sb("st", [P, 6, NT])

        ps = ctx.enter_context(nc.psum_tensor("ps", [128, 8, 512], F32))
        embt_ps = ps[0:T * 10, 6, 0:P]
        h_ps = ps[0:P, 6, 128:128 + T * 2 * J]
        ht_ps = ps[0:S * J, 7, :].bitcast(BF16)[:, 0:T * (P + 1)].rearrange("r (t e) -> r t e", t=T)[:, :, 0:P]
        node_ps = ps[0:D, 5, 384:384 + WIN]
        sum1 = ps[0:P, 4, 0:T * O1 * W].rearrange("p (t g w) -> p t g w", t=T, g=O1)
        sum2 = ps[0:P, 5, 0:T * O2 * W].rearrange("p (t g w) -> p t g w", t=T, g=O2)

        consts_loaded = sem("consts_loaded")
        nodes_loaded = sem("nodes_loaded")
        edges_loaded = sem("edges_loaded")
        pool_consts = sem("pool_consts")
        zeroed = sem("zeroed")
        consts_ready = sem("consts_ready")
        setup_step = sem("setup_step")
        norm_ready = sem("norm_ready")
        geo_ready = sem("geo_ready")
        geo_stored = sem("geo_stored")
        misfit_parts = sem("misfit_parts")
        misfit_sum = sem("misfit_sum")
        misfits_ready = sem("misfits_ready")
        idx_loaded = [sem(f"idx_loaded{n}") for n in range(RING)]
        emb_loaded = [sem(f"emb_loaded{n}") for n in range(RING)]
        geo_loaded = [sem(f"geo_loaded{n}") for n in range(RING)]
        gathered = [sem(f"gathered{n}") for n in range(RING)]
        gather_turn = sem("gather_turn")
        embt_done = sem("embt_done")
        embt_copied = sem("embt_copied")
        h_done = sem("h_done")
        h_ready = sem("h_ready")
        part_ready = [sem(f"part_ready{n}") for n in range(3)]
        rest_ready = sem("rest_ready")
        ht_done = [sem(f"ht_done{n}") for n in range(2)]
        ht_copied = [sem(f"ht_copied{n}") for n in range(2)]
        f1_copied = sem("f1_copied")
        f1_scratch = sem("f1_scratch")
        f1_made = sem("f1_made")
        f2_copied = sem("f2_copied")
        f2_step = sem("f2_step")
        w1_done = sem("w1_done")
        w2_done = sem("w2_done")
        p1_done = sem("p1_done")
        p2_done = sem("p2_done")
        half1_done = sem("half1_done")
        sum1_done = sem("sum1_done")
        sum2_done = sem("sum2_done")
        tanh_done = sem("tanh_done")
        out_step = sem("out_step")
        eo_done = sem("eo_done")
        eo_kept = [sem(f"eo_kept{n}") for n in range(2)]
        far_done = sem("far_done")
        oh_done = sem("oh_done")
        node_done = sem("node_done")
        acc_done = sem("acc_done")
        fb_loaded = sem("fb_loaded")
        fb_step = sem("fb_step")
        fb_turn = sem("fb_turn")
        fb_oh = sem("fb_oh")
        fb_mm = sem("fb_mm")
        sums_ready = sem("sums_ready")
        nodes_turned = sem("nodes_turned")
        ln_step = sem("ln_step")
        var_ready = sem("var_ready")
        std_ready = sem("std_ready")
        y_ready = sem("y_ready")
        stored = sem("stored")

        block = ctx.enter_context(nc.Block())

        HEAD = 5
        TURNS = (NB - 2 - HEAD) // RING

        def steps(eng, step, lead):
            for c in range(HEAD):
                step(Block(0, c))
            with eng.Fori(0, TURNS) as turn:
                for c in range(HEAD, HEAD + RING):
                    step(Block(turn, c))
            for c in range(HEAD + RING * TURNS, NB + lead):
                step(Block(0, c))

        @block.sync
        def _(sp):
            sp.dma_start(vec_b[:], vec.rearrange("(b e) k -> b e k", b=NB)).then_inc(edges_loaded, 16)
            sp.dma_start(dst_b[:], dst.rearrange("(b e) -> b e", b=NB)).then_inc(edges_loaded, 16)
            sp.dma_start(wgt_b[:], weight.rearrange("(b e) -> b e", b=NB)).then_inc(edges_loaded, 16)

            def load(b):
                n = b.c % RING
                if b.known >= RING:
                    sp.wait_ge(gathered[n], b.turns(2 * T * 16))
                at = b.times(BE)
                sp.dma_start(src_r[n][:], src[bass.ds(at, BE)].rearrange("(p t) -> p t", t=T)).then_inc(idx_loaded[n], 16)
                sp.dma_start(dst_r[n][:], dst[bass.ds(at, BE)].rearrange("(p t) -> p t", t=T)).then_inc(idx_loaded[n], 16)
                if b.known >= RING:
                    sp.wait_ge(embt_done, b.times(1, 1 - RING))
                sp.dma_start(emb_r[n][:], emb[bass.ds(at, BE), :].rearrange("(p t) k -> p (t k)", t=T)).then_inc(emb_loaded[n], 16)

            def load_geo(b):
                n = b.c % RING
                if b.known >= RING:
                    sp.wait_ge(eo_done, b.times(1, 1 - RING))
                    sp.wait_ge(far_done, b.times(1, 1 - RING))
                sp.dma_start(geo_r[n][:], geo_dram[bass.ds(b.times(BE), BE), :].rearrange("(p t) k -> p t k", t=T)).then_inc(geo_loaded[n], 16)

            def keep(b):
                sp.wait_ge(eo_done, b.times(1, 1))
                sp.dma_start(eo_all[:, bass.ds(b.times(1), 1), :], eo_r[b.c % 2][:].rearrange("p t d -> p (t d)").unsqueeze(1)).then_inc(eo_kept[b.c % 2], 16)

            for c in range(RING):
                load(Block(0, c))
            sp.wait_ge(zeroed, 1)
            for t in range(T):
                for n, w in enumerate((w11, w21)):
                    sp.dma_start(w1bd[10 * t:10 * t + 10, t, n, :], w).then_inc(consts_loaded, 16)
            for n in range(S):
                rows = slice(J * n, J * n + J)
                for to, of, cols in ((0, 128, 128), (128, 0, 128), (256, 256, 256)):
                    sp.dma_start(w2f[rows, to:to + cols], w12[:, of:of + cols]).then_inc(consts_loaded, 16)
                for to, of, cols in ((0, 64, 64), (64, 192, 64), (128, 0, 64), (192, 128, 64), (256, 256, 128)):
                    sp.dma_start(w2f[rows, C1 + to:C1 + to + cols], w22[:, of:of + cols]).then_inc(consts_loaded, 16)
            sp.dma_start(bases[:], dst.rearrange("(b e) -> e b", b=NB)[0:1, :],
                         allow_slow_non_contiguous=True).then_inc(consts_loaded, 16)
            sp.dma_start(xn[:], x.rearrange("(p m) d -> p m d", p=P)).then_inc(nodes_loaded, 16)
            sp.wait_ge(geo_ready, 1)
            sp.dma_start(geo_dram.rearrange("(b e) k -> b e k", b=NB), geo_b[:]).then_inc(geo_stored, 16)
            sp.wait_ge(geo_stored, 16)
            for c in range(RING):
                load_geo(Block(0, c))
            load(Block(0, RING))
            load(Block(0, RING + 1))

            def step(b):
                if (b + 6).real:
                    load(b + 6)
                if (b + RING).real:
                    load_geo(b + RING)
                if b.real:
                    keep(b)

            for c in range(3):
                step(Block(0, c))
            turns = (NB - 6 - 3) // RING
            with sp.Fori(0, turns) as turn:
                for c in range(3, 3 + RING):
                    step(Block(turn, c))
            for c in range(3 + RING * turns, NB):
                step(Block(0, c))

            sp.wait_ge(misfits_ready, 1)
            flag = sp.value_load(misfits[0:1, 0:1], min_val=0, max_val=2 * NB)
            with sp.If(flag):
                sp.dma_start(dst_all[:], dst.rearrange("(b p t) -> p b t", p=P, t=T)).then_inc(fb_loaded, 16)
            with sp.Else():
                sp.nop()
            sp.wait_ge(y_ready, 1)
            sp.dma_start(out.rearrange("(p m) d -> p m d", p=P), yn[:]).then_inc(stored, 16)
            sp.wait_ge(stored, 16)
            for n in range(2):
                sp.wait_ge(eo_kept[n], 16 * len(range(n, NB, 2)))

        @block.gpsimd
        def _(pool):
            nc.gpsimd.memset(w1bd[:].rearrange("r t n j -> r (t n j)"), 0.0).then_inc(zeroed, 1)
            nc.gpsimd.memset(ones[:], 1.0).then_inc(pool_consts, 1)
            nc.gpsimd.iota(iota_i[:], pattern=[[1, P]], base=0, channel_multiplier=0).then_inc(pool_consts, 1)
            nc.gpsimd.memset(ident[:], 0.0).then_inc(pool_consts, 1)
            pool.wait_ge(pool_consts, 3)
            nc.gpsimd.affine_select(out=ident[:], in_=ident[:], compare_op=ALU.not_equal, fill=1.0, base=0,
                                    pattern=[[-1, 128]], channel_multiplier=1).then_inc(pool_consts, 1)

            def step(b):
                n = b.c % RING
                if not b.real:
                    return
                pool.wait_ge(idx_loaded[n], b.turns(32, 32))
                if b.known >= RING:
                    pool.wait_ge(f1_copied, b.times(5, 5 - 5 * RING))
                pool.sem_inc(gather_turn, 1)
                for t in range(T):
                    for k, idx in enumerate((src_r[n], dst_r[n])):
                        nc.gpsimd.indirect_dma_start(
                            x_r[n][:, t, k, :], None, x, bass.IndirectOffsetOnAxis(idx[:, t:t + 1], axis=0)
                        ).then_inc(gathered[n], 16)

            steps(pool, step, 0)

        @block.scalar
        def _(act):
            act.wait_ge(setup_step, 2)
            nc.scalar.activation(nrm_b[:], n2_b[:], ACT.Sqrt).then_inc(norm_ready, 1)

            def f1_copies(b):
                n, f1 = b.c % RING, f1_r[b.c % 2]
                act.wait_ge(gathered[n], b.turns(2 * T * 16, 2 * T * 16))
                if b.known >= 2:
                    act.wait_ge(p1_done, b.times(2 * T, -2 * T))
                xs = x_r[n][:]
                for k, of in ((1, xs[:, :, :, 0:8]), (2, xs[:, :, :, 0:8])) + tuple(
                        (3 + k, xs[:, :, :, 8 + k:D:3]) for k in range(3)):
                    nc.scalar.copy(f1[:, :, k, :].rearrange("p t (h u) -> p t h u", h=2), of).then_inc(f1_copied, 1)

            def f2_copies(b):
                act.wait_ge(sum1_done, b.times(1, 1))
                if b.known >= 2:
                    act.wait_ge(p2_done, b.times(2 * T, -2 * T))
                nc.scalar.copy(f2_r[b.c % 2][:, :, 2:5, :],
                               sum1[:, :, 0:1, :].to_broadcast([P, T, 3, W])).then_inc(f2_copied, 1)

            def one_hot(b):
                n = b.c % RING
                act.wait_ge(geo_loaded[n], b.turns(16, 16))
                if b.known >= 1:
                    act.wait_ge(oh_done, b.times(1))
                for t in range(T):
                    last = nc.scalar.activation(far[:, t, :], iota[:, 0:WIN], ACT.Abs, bias=geo_r[n][:, t, 3:4])
                last.then_inc(far_done, 1)
                act.wait_ge(far_done, b.times(1, 1))
                if b.known >= 2:
                    act.wait_ge(node_done, b.times(1, -1))
                nc.scalar.activation(oh_r[b.c % 2][:], far[:], ACT.Relu, scale=-1.0, bias=ones[:]).then_inc(oh_done, 1)

            def tanhs(b):
                if b.known >= 2:
                    act.wait_ge(eo_done, b.times(1, -1))
                act.wait_ge(sum2_done, b.times(1, 1))
                nc.scalar.activation(th_r[b.c % 2][:], sum2[:, :, 0:2, :], ACT.Tanh).then_inc(tanh_done, 1)

            def hidden(b):
                act.wait_ge(h_done, b.times(1, 1))
                if b.known >= 2:
                    act.wait_ge(part_ready[2], b.times(1, -1))
                nc.scalar.activation(h_r[b.c % 2][:].rearrange("p t n j -> p (t n j)"), h_ps, ACT.Relu,
                                     scale=1.0 / math.sqrt(10.0)).then_inc(h_ready, 1)

            def h_part(b, part):
                slots = [n for n, (k, _) in enumerate(SLOTS) if k == part]
                if part == 0:
                    act.wait_ge(h_ready, b.times(1, 1))
                    if b.known >= 2:
                        act.wait_ge(ht_done[1], b.times(1, -1))
                else:
                    act.wait_ge(rest_ready, b.times(2, part))
                hp, h = hp_r[b.c % 2], h_r[b.c % 2]
                for k in range(2):
                    last = nc.scalar.copy(hp[:, k, :, slots[0]:slots[-1] + 1, :],
                                          h[:, :, k, :].unsqueeze(2).to_broadcast([P, T, len(slots), J]))
                last.then_inc(part_ready[part], 1)

            def ht_copy(b, k):
                used, per = (w1_done, T) if k == 0 else (w2_done, T)
                if b.known >= 2:
                    act.wait_ge(used, b.times(per, -per))
                act.wait_ge(ht_done[k], b.times(1, 1))
                nc.scalar.copy(ht_r[k][b.c % 2][:].rearrange("r (t e) -> r t e", t=T), ht_ps).then_inc(ht_copied[k], 1)

            def embt_copy(b):
                if b.known >= 2:
                    act.wait_ge(h_done, b.times(1, -1))
                act.wait_ge(embt_done, b.times(1, 1))
                nc.scalar.copy(embt_r[b.c % 2][:], embt_ps).then_inc(embt_copied, 1)

            def step(b):
                if (b + -1).real:
                    f2_copies(b + -1)
                if (b + 2).real:
                    embt_copy(b + 2)
                if (b + 1).real:
                    f1_copies(b + 1)
                    ht_copy(b + 1, 0)
                if (b + 2).real:
                    hidden(b + 2)
                    h_part(b + 2, 0)
                if (b + -2).real:
                    one_hot(b + -2)
                    tanhs(b + -2)
                if (b + 1).real:
                    ht_copy(b + 1, 1)
                if (b + 2).real:
                    h_part(b + 2, 1)
                    h_part(b + 2, 2)

            act.wait_ge(consts_ready, 3)
            step(Block(0, -2))
            step(Block(0, -1))
            steps(act, step, 3)
            act.wait_ge(var_ready, 1)
            nc.scalar.activation(st[:, 2, :], st[:, 1, :], ACT.Sqrt).then_inc(std_ready, 1)

        @block.vector
        def _(dve):
            setup = [0]

            def link(ins):
                setup[0] += 1
                ins.then_inc(setup_step, 1)
                dve.wait_ge(setup_step, setup[0])

            dve.wait_ge(edges_loaded, 48)
            link(nc.vector.tensor_tensor(geo_b[:, :, 0:3], vec_b[:], vec_b[:], ALU.mult))
            link(nc.vector.tensor_reduce(n2_b[:], geo_b[:, :, 0:3], AX.X, ALU.add))
            nc.vector.memset(acc[:], 0.0)
            link(nc.vector.tensor_copy(dstf_b[:], dst_b[:]))
            link(nc.vector.tensor_scalar(geo_b[:, :, 3], dstf_b[:], -1.0, dstf_b[:, 0:1], ALU.mult, ALU.add))
            link(nc.vector.tensor_copy(geo_b[:, :, 4], wgt_b[:]))
            dve.wait_ge(norm_ready, 1)
            link(nc.vector.reciprocal(inv_b[:], nrm_b[:]))
            link(nc.vector.tensor_tensor(dstf_b[:], n2_b[:], inv_b[:], ALU.mult))
            link(nc.vector.tensor_tensor(dstf_b[:], dstf_b[:], inv_b[:], ALU.mult))
            link(nc.vector.tensor_scalar(dstf_b[:], dstf_b[:], -0.5, 1.5, ALU.mult, ALU.add))
            link(nc.vector.tensor_tensor(inv_b[:], inv_b[:], dstf_b[:], ALU.mult))
            nc.vector.tensor_tensor(geo_b[:, :, 0:3], vec_b[:], inv_b[:].unsqueeze(2).to_broadcast([NB, BE, 3]),
                                    ALU.mult).then_inc(geo_ready, 1)
            dve.wait_ge(pool_consts, 4)
            nc.vector.tensor_copy(iota[:], iota_i[:]).then_inc(consts_ready, 1)
            nc.vector.tensor_copy(ident_h[:], ident[0:P, 0:P]).then_inc(consts_ready, 1)
            dve.wait_ge(consts_loaded, 16 * (2 * T + 8 * S + 1))
            c1, c2 = 0.25 / math.sqrt(32.0), 1.0 / 16.0
            for a, b, c in ((0, 256, c1), (256, 384, c1 * SQRT3), (384, C1, c1),
                            (C1, C1 + 256, c2), (C1 + 256, C1 + 320, c2 * SQRT3), (C1 + 320, C1 + C2, c2)):
                link(nc.vector.tensor_scalar(w2f[:, a:b], w2f[:, a:b], c, None, ALU.mult))
            for n in range(3):
                link(nc.vector.tensor_copy(w2part[n][:], w2f[:]))
                if n < 2:
                    link(nc.vector.tensor_tensor(w2f[:], w2f[:], w2part[n][:], ALU.subtract))
            rows = ident[0:S * J, 0:S * J].rearrange("p (s j) -> p s j", s=S)
            for n, (a, b, c) in enumerate(((0, 4, 3), (1, 5, 3), (2, 3, 1), (5, 6, 1))):
                link(nc.vector.tensor_reduce(slot_mask[:, n:n + 1], rows[:, a:b:c, :], AX.XY, ALU.add))
            link(nc.vector.tensor_tensor(slot_mask[:, 0:1], slot_mask[:, 0:1], slot_mask[:, 3:4], ALU.add))
            link(nc.vector.tensor_scalar(w2s[:], w2part[0][:], slot_mask[:, 0:1], None, ALU.mult))
            for n in (1, 2):
                last = nc.vector.scalar_tensor_tensor(out=w2s[:], in0=w2part[n][:], scalar=slot_mask[:, n:n + 1],
                                                      in1=w2s[:], op0=ALU.mult, op1=ALU.add)
                if n == 1:
                    link(last)
            last.then_inc(consts_ready, 1)
            link(nc.vector.tensor_reduce(ext[:, 0:1], geo_b[:, :, 3], AX.X, ALU.max))
            link(nc.vector.tensor_reduce(ext[:, 1:2], geo_b[:, :, 3], AX.X, ALU.min))
            link(nc.vector.tensor_scalar(ext[:, 0:1], ext[:, 0:1], 0.0, None, ALU.is_gt))
            link(nc.vector.tensor_scalar(ext[:, 1:2], ext[:, 1:2], 1.0 - WIN, None, ALU.is_lt))
            nc.vector.tensor_tensor(ext[:, 2:3], ext[:, 0:1], ext[:, 1:2], ALU.add).then_inc(misfit_parts, 1)
            dve.wait_ge(misfit_sum, 1)
            nc.vector.tensor_copy(misfits[:], ps[0:1, 0, 0:1]).then_inc(misfits_ready, 1)

            def directions(b, v):
                return geo_r[b.c % RING][:, :, 0:3].unsqueeze(3).to_broadcast([P, T, 3, v])

            def f1_make(b):
                n, f1 = b.c % RING, f1_r[b.c % 2]
                dve.wait_ge(geo_loaded[n], b.turns(16, 16))
                dve.wait_ge(f1_copied, b.times(5, 5))
                nc.vector.tensor_tensor(tmp1[:], f1[:, :, 3:6, :], directions(b, V1), ALU.mult).then_inc(f1_scratch, 1)
                dve.wait_ge(f1_scratch, b.times(1, 1))
                nc.vector.tensor_reduce(f1[:, :, 0, :], tmp1[:].rearrange("p t k u -> p t u k"), AX.X,
                                        ALU.add).then_inc(f1_made, 1)

            def f2_make(b):
                f2, dirs = f2_r[b.c % 2], directions(b, W)
                dve.wait_ge(f2_copied, b.times(1, 1))
                nc.vector.tensor_tensor(tmp2[:], sum1[:, :, 1:2, :].to_broadcast([P, T, 3, W]), dirs,
                                        ALU.mult).then_inc(f2_step, 1)
                dve.wait_ge(f2_step, b.times(5, 1))
                nc.vector.tensor_tensor(f2[:, :, 5:8, :], tmp2[:], sum1[:, :, 2:5, :], ALU.add).then_inc(f2_step, 1)
                dve.wait_ge(f2_step, b.times(5, 2))
                nc.vector.tensor_tensor(tmp3[:], f2[:, :, 5:8, :], dirs, ALU.mult).then_inc(f2_step, 1)
                dve.wait_ge(f2_step, b.times(5, 3))
                for k in range(2):
                    nc.vector.tensor_reduce(f2[:, :, k, :], tmp3[:].rearrange("p t k u -> p t u k"), AX.X,
                                            ALU.add).then_inc(f2_step, 1)

            def products1(b):
                f1, p1 = f1_r[b.c % 2], p1_r[b.c % 2]
                dve.wait_ge(f1_made, b.times(1, 1))
                if b.known >= 2:
                    dve.wait_ge(sum1_done, b.times(1, -1))
                for t in range(T):
                    wps = ps[0:P, (b.c + t) % 2, :].rearrange("p (g u w) -> p g u w", g=4, w=W)
                    dve.wait_ge(w1_done, b.times(T, t + 1))
                    nc.vector.tensor_tensor(p1[:, :, t, 0:3, :].rearrange("p u g w -> p g u w"), wps[:, 0:3],
                                            f1[:, t, 0:3, :].unsqueeze(3).to_broadcast([P, 3, V1, W]),
                                            ALU.mult).then_inc(p1_done, 1)
                    nc.vector.tensor_tensor(p1[:, :, t, 3:6, :].rearrange("p u g w -> p g u w"),
                                            wps[:, 3:4].to_broadcast([P, 3, V1, W]),
                                            f1[:, t, 3:6, :].unsqueeze(3).to_broadcast([P, 3, V1, W]),
                                            ALU.mult).then_inc(p1_done, 1)

            def halve1(b):
                p1 = p1_r[b.c % 2]
                dve.wait_ge(p1_done, b.times(2 * T, 2 * T))
                lo, hi = (p1[:, a:a + HALF1].rearrange("p u t g w -> p (u t g w)") for a in (0, V1 - HALF1))
                nc.vector.tensor_tensor(lo, lo, hi, ALU.add).then_inc(half1_done, 1)

            def products2(b):
                f2, p2 = f2_r[b.c % 2], p2_r[b.c % 2]
                dve.wait_ge(f2_step, b.times(5, 5))
                if b.known >= 2:
                    dve.wait_ge(sum2_done, b.times(1, -1))
                for t in range(T):
                    wps = ps[0:P, 2 + (b.c + t) % 2, 0:C2].rearrange("p (g u w) -> p g u w", g=6, w=W)
                    dve.wait_ge(w2_done, b.times(T, t + 1))
                    nc.vector.tensor_tensor(p2[:, :, t, 0:5, :].rearrange("p u g w -> p g u w"), wps[:, 0:5],
                                            f2[:, t, 0:5, :].unsqueeze(3).to_broadcast([P, 5, V2, W]),
                                            ALU.mult).then_inc(p2_done, 1)
                    nc.vector.tensor_tensor(p2[:, :, t, 5:8, :].rearrange("p u g w -> p g u w"),
                                            wps[:, 5:6].to_broadcast([P, 3, V2, W]),
                                            f2[:, t, 5:8, :].unsqueeze(3).to_broadcast([P, 3, V2, W]),
                                            ALU.mult).then_inc(p2_done, 1)

            def h_rest(b, part):
                dve.wait_ge(part_ready[part], b.times(1, 1))
                slot = [n for n, (k, _) in enumerate(SLOTS) if k == part][0]
                h = h_r[b.c % 2][:]
                nc.vector.tensor_tensor(h, h, hp_r[b.c % 2][:, :, :, slot, :].rearrange("p k t j -> p t k j"),
                                        ALU.subtract).then_inc(rest_ready, 1)

            def output(b):
                th, eo, geo = th_r[b.c % 2], eo_r[b.c % 2], geo_r[b.c % RING]
                wb = geo[:, :, 4:5].to_broadcast([P, T, W])
                dve.wait_ge(tanh_done, b.times(1, 1))
                nc.vector.tensor_tensor(tmp4[:], sum2[:, :, 2:3, :].to_broadcast([P, T, 3, W]), directions(b, W),
                                        ALU.mult).then_inc(out_step, 1)
                nc.vector.tensor_tensor(gate[:], th[:, :, 1, :], wb, ALU.mult).then_inc(out_step, 1)
                dve.wait_ge(out_step, b.times(4, 1))
                nc.vector.tensor_tensor(tmp4[:], tmp4[:], sum2[:, :, 3:6, :], ALU.add).then_inc(out_step, 1)
                if b.known >= 2:
                    dve.wait_ge(node_done, b.times(1, -1))
                    dve.wait_ge(eo_kept[b.c % 2], b.pairs(16))
                nc.vector.tensor_tensor(eo[:, :, 0:8], th[:, :, 0, :], wb, ALU.mult).then_inc(out_step, 1)
                dve.wait_ge(out_step, b.times(4, 4))
                nc.vector.tensor_tensor(eo[:, :, 8:D].rearrange("p t (u k) -> p t k u", k=3), tmp4[:],
                                        gate[:].unsqueeze(2).to_broadcast([P, T, 3, W]), ALU.mult).then_inc(eo_done, 1)

            def accumulate(b):
                base = dve.value_load(bases[0:1, bass.ds(b.times(1), 1)], min_val=0, max_val=N - 1)
                dve.wait_ge(node_done, b.times(1, 1))
                if b.known >= 1:
                    dve.wait_ge(acc_done, b.times(1))
                nodes = acc[:, bass.ds(base, WIN)]
                nc.vector.tensor_tensor(nodes, nodes, node_ps, ALU.add).then_inc(acc_done, 1)

            def step(b):
                if (b + -1).real:
                    f2_make(b + -1)
                if (b + -3).real:
                    accumulate(b + -3)
                if b.real:
                    products1(b)
                    halve1(b)
                if (b + 1).real:
                    f1_make(b + 1)
                if (b + 2).real:
                    h_rest(b + 2, 0)
                if (b + -1).real:
                    products2(b + -1)
                if (b + 2).real:
                    h_rest(b + 2, 1)
                if (b + -2).real:
                    output(b + -2)

            step(Block(0, -2))
            step(Block(0, -1))
            steps(dve, step, 3)

            flag = dve.value_load(misfits[0:1, 0:1], min_val=0, max_val=2 * NB)
            with dve.If(flag):
                dve.wait_ge(fb_loaded, 16)
                dve.wait_ge(acc_done, NB)
                nc.vector.memset(acc[:], 0.0).then_inc(fb_step, 1)
                dve.wait_ge(fb_step, 1)
                with dve.Fori(0, NB) as i:
                    nc.vector.tensor_copy(dst_w[:], dst_all[:, bass.ds(i, 1), :].rearrange("p b t -> p (b t)")).then_inc(fb_step, 1)
                    nc.vector.tensor_copy(eo_s[:].rearrange("p t d -> p (t d)"),
                                          eo_all[:, bass.ds(i, 1), :].rearrange("p b n -> p (b n)")).then_inc(fb_step, 1)
                    dve.wait_ge(fb_step, i * (2 + 2 * NT) + 3)
                    dve.sem_inc(fb_turn, 1)
                    with dve.Fori(0, NT) as m:
                        nc.vector.tensor_tensor(oh_w[:], iota[:].unsqueeze(1).to_broadcast([P, T, P]),
                                                dst_w[:].unsqueeze(2).to_broadcast([P, T, P]), ALU.is_equal).then_inc(fb_oh, 1)
                        dve.wait_ge(fb_oh, i * NT + m + 1)
                        nc.vector.tensor_scalar(dst_w[:], dst_w[:], -float(P), None, ALU.add).then_inc(fb_step, 1)
                        dve.wait_ge(fb_mm, i * NT + m + 1)
                        nodes = acc[:, bass.ds(m * P, P)]
                        nc.vector.tensor_tensor(nodes, nodes, ps[0:D, 0, 0:P], ALU.add).then_inc(fb_step, 1)
                        dve.wait_ge(fb_step, i * (2 + 2 * NT) + m * 2 + 5)
                nc.vector.engine_nop().then_inc(sums_ready, 1)
            with dve.Else():
                dve.wait_ge(acc_done, NB)
                nc.vector.engine_nop().then_inc(sums_ready, 1)

            turned = [0]

            def chain(ins):
                turned[0] += 1
                ins.then_inc(ln_step, 1)
                dve.wait_ge(ln_step, turned[0])

            def wide(a):
                return a.unsqueeze(2).to_broadcast([P, NT, D])

            dve.wait_ge(nodes_loaded, 16)
            dve.wait_ge(nodes_turned, 1)
            chain(nc.vector.tensor_tensor(yn[:].rearrange("p m d -> p (m d)"), xn[:].rearrange("p m d -> p (m d)"),
                                          ps[0:P].rearrange("p b c -> p (b c)")[:, 0:NT * D], ALU.add))
            chain(nc.vector.tensor_reduce(st[:, 0, :], yn[:], AX.X, ALU.add))
            chain(nc.vector.tensor_scalar(st[:, 0, :], st[:, 0, :], 1.0 / D, None, ALU.mult))
            chain(nc.vector.tensor_tensor(yn[:], yn[:], wide(st[:, 0, :]), ALU.subtract))
            chain(nc.vector.tensor_tensor(xn[:], yn[:], yn[:], ALU.mult))
            chain(nc.vector.tensor_reduce(st[:, 5, :], xn[:], AX.X, ALU.add))
            nc.vector.tensor_scalar(st[:, 1, :], st[:, 5, :], 1.0 / D, EPS, ALU.mult, ALU.add).then_inc(var_ready, 1)
            dve.wait_ge(std_ready, 1)
            chain(nc.vector.reciprocal(st[:, 3, :], st[:, 2, :]))
            chain(nc.vector.tensor_tensor(st[:, 4, :], st[:, 3, :], st[:, 1, :], ALU.mult))
            chain(nc.vector.tensor_tensor(st[:, 4, :], st[:, 4, :], st[:, 3, :], ALU.mult))
            chain(nc.vector.tensor_scalar(st[:, 4, :], st[:, 4, :], -0.5, 1.5, ALU.mult, ALU.add))
            chain(nc.vector.tensor_tensor(st[:, 3, :], st[:, 3, :], st[:, 4, :], ALU.mult))
            nc.vector.tensor_tensor(yn[:], yn[:], wide(st[:, 3, :]), ALU.mult).then_inc(y_ready, 1)

        @block.tensor
        def _(pe):
            idn = ident[0:P, 0:P]
            pe.wait_ge(pool_consts, 4)
            pe.wait_ge(misfit_parts, 1)
            nc.tensor.matmul(ps[0:1, 0, 0:1], ext[:, 2:3], ones[0:NB, :], start=True, stop=True).then_inc(misfit_sum, 1)
            pe.wait_ge(misfits_ready, 1)
            pe.wait_ge(consts_ready, 3)

            def ht(b, k):
                pe.wait_ge(part_ready[2], b.times(1, 1))
                if k == 1:
                    pe.wait_ge(ht_copied[0], b.times(1, 1))
                elif b.known >= 1:
                    pe.wait_ge(ht_copied[1], b.times(1))
                for t in range(T):
                    last = nc.tensor.transpose(ht_ps[:, t, :],
                                               hp_r[b.c % 2][:, k, t].rearrange("p s j -> p (s j)"), ident_h[:])
                last.then_inc(ht_done[k], 1)

            def w(b, t, k, p_done, w_done):
                if t == 0:
                    pe.wait_ge(ht_copied[k], b.times(1, 1))
                if b.known >= 1 or t >= 2:
                    pe.wait_ge(p_done, b.times(2 * T, 2 * (t - 1)))
                cols = slice(0, C1) if k == 0 else slice(C1, C1 + C2)
                nc.tensor.matmul(ps[0:P, 2 * k + (b.c + t) % 2, 0:C1 if k == 0 else C2],
                                 ht_r[k][b.c % 2][:, P * t:P * t + P], w2s[:, cols],
                                 start=True, stop=True).then_inc(w_done, 1)

            def sums(part, left, p, twice, dest):
                kinds = p.shape[3]
                for u in range(left * part // T, left * (part + 1) // T):
                    nc.tensor.matmul(dest, idn, p[:, u, :, twice:kinds, :], start=(u == 0), stop=False)
                    last = nc.tensor.matmul(dest[:, :, 0:twice, :], idn, p[:, u, :, 0:twice, :],
                                            start=False, stop=(u == left - 1))
                return last

            def sum_1(b, part):
                if part == 0:
                    pe.wait_ge(half1_done, b.times(1, 1))
                    if b.known >= 1:
                        pe.wait_ge(f2_step, b.times(5, -3))
                last = sums(part, V1 - HALF1, p1_r[b.c % 2], 1, sum1)
                if part == T - 1:
                    last.then_inc(sum1_done, 1)

            def sum_2(b, part):
                if part == 0:
                    pe.wait_ge(p2_done, b.times(2 * T, 2 * T))
                    if b.known >= 1:
                        pe.wait_ge(eo_done, b.times(1))
                        pe.wait_ge(acc_done, b.times(1))
                last = sums(part, V2, p2_r[b.c % 2], 2, sum2)
                if part == T - 1:
                    last.then_inc(sum2_done, 1)

            def over_nodes(b):
                pe.wait_ge(oh_done, b.times(1, 1))
                pe.wait_ge(eo_done, b.times(1, 1))
                for t in range(T):
                    last = nc.tensor.matmul(node_ps, eo_r[b.c % 2][:, t, :], oh_r[b.c % 2][:, t, :],
                                            start=(t == 0), stop=(t == T - 1))
                last.then_inc(node_done, 1)

            def step(b):
                if (b + -3).real:
                    over_nodes(b + -3)
                for t in range(T):
                    if b.real:
                        w(b, t, 0, p1_done, w1_done)
                    if t == 0 and (b + 2).real:
                        n, a = (b.c + 2) % RING, b + 2
                        pe.wait_ge(emb_loaded[n], a.turns(16, 16))
                        if a.known >= 1:
                            pe.wait_ge(h_ready, a.times(1))
                        nc.tensor.matmul(embt_ps, emb_r[n][:], idn, start=True, stop=True).then_inc(embt_done, 1)
                    if t == 2 and (b + 1).real:
                        ht(b + 1, 0)
                    if t >= 1 and (b + -2).real:
                        sum_2(b + -2, t - 1)
                if (b + -2).real:
                    sum_2(b + -2, T - 1)
                if (b + 2).real:
                    a = b + 2
                    pe.wait_ge(embt_copied, a.times(1, 1))
                    nc.tensor.matmul(h_ps, embt_r[a.c % 2][:], w1bd[:].rearrange("r t n j -> r (t n j)"),
                                     start=True, stop=True).then_inc(h_done, 1)
                for t in range(T):
                    if (b + -1).real:
                        w(b + -1, t, 1, p2_done, w2_done)
                    if t == 2 and (b + 1).real:
                        ht(b + 1, 1)
                    if t >= 1 and b.real:
                        sum_1(b, t - 1)
                if b.real:
                    sum_1(b, T - 1)

            step(Block(0, -2))
            step(Block(0, -1))
            steps(pe, step, 3)

            flag = pe.value_load(misfits[0:1, 0:1], min_val=0, max_val=2 * NB)
            with pe.If(flag):
                with pe.Fori(0, NB) as i:
                    with pe.Fori(0, NT) as m:
                        pe.wait_ge(fb_oh, i * NT + m + 1)
                        for t in range(T):
                            last = nc.tensor.matmul(ps[0:D, 0, 0:P], eo_s[:, t, :], oh_w[:, t, :],
                                                    start=(t == 0), stop=(t == T - 1))
                        last.then_inc(fb_mm, 1)
            with pe.Else():
                pe.nop()
            pe.wait_ge(sums_ready, 1)
            for m in range(NT):
                b, at = divmod(m * D, 512)
                last = nc.tensor.transpose(ps[0:P, b, at:at + D], acc[:, m:N:NT], ident[0:D, 0:D])
            last.then_inc(nodes_turned, 1)


def kernel(x, src, dst, edge_attr_10, edge_attr_3, edge_weight,
           L0_gnn_fc1_w1, L0_gnn_fc1_w2, L0_gnn_fc2_w1, L0_gnn_fc2_w2):
    import numpy as np
    import concourse.bacc as bacc
    from concourse.bass_utils import run_bass_kernel_spmd

    nc = bacc.Bacc("TRN2", target_bir_lowering=False, num_devices=1)
    given = {"x": x, "src": src, "dst": dst, "emb": edge_attr_10, "vec": edge_attr_3, "weight": edge_weight,
             "w11": L0_gnn_fc1_w1, "w12": L0_gnn_fc1_w2, "w21": L0_gnn_fc2_w1, "w22": L0_gnn_fc2_w2}
    arrays, args = {}, {}
    for name, a in given.items():
        a = np.ascontiguousarray(a)
        arrays[f"in_{name}"] = a
        args[name] = nc.dram_tensor(f"in_{name}", a.shape, mybir.dt.from_np(a.dtype), kind="ExternalInput").ap()
    args["out"] = nc.dram_tensor("out_y", (N, D), F32, kind="ExternalOutput").ap()
    program(nc, **args)
    r = run_bass_kernel_spmd(nc, [arrays], core_ids=[0])
    return r.results[0]["out_y"]
```

```python
import math
from contextlib import ExitStack

import concourse.bass as bass
from concourse import mybir

F32 = mybir.dt.float32
BF16 = mybir.dt.bfloat16
I32 = mybir.dt.int32
ALU = mybir.AluOpType
ACT = mybir.ActivationFunctionType
AX = mybir.AxisListType

N = 3125
E = 53125
D = 32
P = 125
T = 5
BE = P * T
NB = E // BE
J = 16
W = 8
V1 = 16
V2 = 8
K1 = 6
K2 = 8
C1 = 4 * V1 * W
C2 = 6 * V2 * W
WIN = 64
HALF1 = 5
SLOTS = ((0, 0), (0, 1), (0, 2), (1, 0), (1, 1), (2, 0))
S = len(SLOTS)
NT = N // P
RING = 4
GROUPS = (((0, 2, 0), (2, 2, 2), (4, 1, 0)), ((0, 2, 2), (2, 2, 0), (4, 1, 2)))
NG = len(GROUPS[0])
SQRT3 = math.sqrt(3.0)
EPS = 1e-5


class Block:

    def __init__(self, turn, c):
        self.turn, self.c = turn, c

    def __add__(self, d):
        return Block(self.turn, self.c + d)

    def times(self, k, plus=0):
        if isinstance(self.turn, int):
            return k * (RING * self.turn + self.c) + plus
        return self.turn * (RING * k) + (k * self.c + plus)

    def turns(self, k, plus=0):
        return self.turn * k + (k * (self.c // RING) + plus)

    def pairs(self, k, plus=0):
        return self.turn * (RING // 2 * k) + (k * (self.c // 2) + plus)

    @property
    def known(self):
        return self.c if isinstance(self.turn, int) else min(max(self.c, RING), NB - RING)

    @property
    def real(self):
        return 0 <= self.c < NB or not isinstance(self.turn, int)


def program(nc, x, src, dst, emb, vec, weight, w11, w12, w21, w22, out):
    ctx = ExitStack()
    with ctx:
        def sb(name, shape, dt=F32):
            return ctx.enter_context(nc.sbuf_tensor(name, shape, dt))

        def sem(name):
            return ctx.enter_context(nc.semaphore(name))

        ident = sb("ident", [128, 128])
        iota_i = sb("iota_i", [P, P], I32)
        iota = sb("iota", [P, P])
        ones = sb("ones", [P, 1])
        slot_mask = sb("slot_mask", [S * J, 4])
        w2f = sb("w2f", [S * J, C1 + C2])
        w2part = [sb(f"w2part{n}", [S * J, C1 + C2], BF16) for n in range(3)]
        w2s = sb("w2s", [S * J, C1 + C2], BF16)
        w1bd = sb("w1bd", [T * 10, T, 2, J])
        ident_h = sb("ident_h", [P, P], BF16)
        vec_b = sb("vec_b", [NB, BE, 3])
        dst_b = sb("dst_b", [NB, BE], I32)
        dstf_b = sb("dstf_b", [NB, BE])
        wgt_b = sb("wgt_b", [NB, BE])
        n2_b = sb("n2_b", [NB, BE])
        nrm_b = sb("nrm_b", [NB, BE])
        inv_b = sb("inv_b", [NB, BE])
        geo_b = sb("geo_b", [NB, BE, 5])
        ext = sb("ext", [NB, 4])
        misfits = sb("misfits", [1, 1], I32)
        bases = sb("bases", [1, NB], I32)
        geo_dram = nc.dram_tensor("geo_dram", (E, 5), F32, kind="Internal").ap()
        src_r = [sb(f"src{n}", [P, T], I32) for n in range(RING)]
        dst_r = [sb(f"dst{n}", [P, T], I32) for n in range(RING)]
        emb_r = [sb(f"emb{n}", [P, T * 10]) for n in range(RING)]
        geo_r = [sb(f"geo{n}", [P, T, 5]) for n in range(RING)]
        x_r = [sb(f"x{n}", [P, T, 2, D]) for n in range(RING)]
        h_r = [sb(f"h{n}", [P, T, 2, J]) for n in range(2)]
        hp_r = [sb(f"hp{n}", [P, 2, T, S, J], BF16) for n in range(2)]
        ht_r = [[sb(f"ht{k}_{n}", [S * J, T * P], BF16) for n in range(2)] for k in range(2)]
        f1_r = [sb(f"f1_{n}", [P, T, K1, V1]) for n in range(2)]
        f2_r = [sb(f"f2_{n}", [P, T, K2, V2]) for n in range(2)]
        embt_r = [sb(f"embt{n}", [T * 10, P]) for n in range(2)]
        p1_r = [sb(f"p1_{n}", [P, T, K1, V1, W]) for n in range(2)]
        p2_r = [sb(f"p2_{n}", [P, T, K2, V2, W]) for n in range(2)]
        th_r = [sb(f"th{n}", [P, T, 2, W]) for n in range(2)]
        eo_r = [sb(f"eo{n}", [P, T, D]) for n in range(2)]
        oh_r = [sb(f"oh{n}", [P, T, WIN]) for n in range(2)]
        far = sb("far", [P, T, WIN])
        tmp1 = sb("tmp1", [P, T, 3, V1])
        tmp2 = sb("tmp2", [P, T, 3, W])
        tmp3 = sb("tmp3", [P, T, 3, W])
        tmp4 = sb("tmp4", [P, T, 3, W])
        tmp5 = sb("tmp5", [P, T, W])
        pre_r = [sb(f"pre{n}", [P, T, 2, W]) for n in range(2)]
        gate = sb("gate", [P, T, W])
        acc = sb("acc", [D, N + WIN])
        eo_all = sb("eo_all", [P, NB, T * D])
        eo_s = sb("eo_s", [P, T, D])
        dst_all = sb("dst_all", [P, NB, T], I32)
        dst_w = sb("dst_w", [P, T])
        oh_w = sb("oh_w", [P, T, P])
        xn = sb("xn", [P, NT, D])
        yn = sb("yn", [P, NT, D])
        st = sb("st", [P, 6, NT])

        ps = ctx.enter_context(nc.psum_tensor("ps", [128, 8, 512], F32))
        embt_ps = ps[0:T * 10, 6, 0:P]
        h_ps = ps[0:P, 6, 128:128 + T * 2 * J]
        ht_ps = ps[0:S * J, 7, :].bitcast(BF16)[:, 0:T * (P + 1)].rearrange("r (t e) -> r t e", t=T)[:, :, 0:P]
        node_ps = ps[0:D, 7, 384:384 + WIN]
        sum1 = ps[0:P, 4, 0:T * K1 * W].rearrange("p (t g w) -> p t g w", t=T, g=K1)
        sum2 = ps[0:P, 5, 0:T * K2 * W].rearrange("p (t g w) -> p t g w", t=T, g=K2)

        consts_loaded = sem("consts_loaded")
        nodes_loaded = sem("nodes_loaded")
        edges_loaded = sem("edges_loaded")
        pool_consts = sem("pool_consts")
        zeroed = sem("zeroed")
        consts_ready = sem("consts_ready")
        setup_step = sem("setup_step")
        norm_ready = sem("norm_ready")
        geo_ready = sem("geo_ready")
        geo_stored = sem("geo_stored")
        misfit_parts = sem("misfit_parts")
        misfit_sum = sem("misfit_sum")
        misfits_ready = sem("misfits_ready")
        idx_loaded = [sem(f"idx_loaded{n}") for n in range(RING)]
        emb_loaded = [sem(f"emb_loaded{n}") for n in range(RING)]
        geo_loaded = [sem(f"geo_loaded{n}") for n in range(RING)]
        gathered = [sem(f"gathered{n}") for n in range(RING)]
        gather_turn = sem("gather_turn")
        embt_done = sem("embt_done")
        embt_copied = sem("embt_copied")
        h_done = sem("h_done")
        h_ready = sem("h_ready")
        part_ready = [sem(f"part_ready{n}") for n in range(3)]
        rest_ready = sem("rest_ready")
        ht_done = [sem(f"ht_done{n}") for n in range(2)]
        ht_copied = [sem(f"ht_copied{n}") for n in range(2)]
        f1_copied = sem("f1_copied")
        f1_scratch = sem("f1_scratch")
        f1_made = sem("f1_made")
        f2_step = sem("f2_step")
        w1_done = sem("w1_done")
        w2_done = sem("w2_done")
        p1_done = sem("p1_done")
        p2_done = sem("p2_done")
        half1_done = sem("half1_done")
        sum1_done = sem("sum1_done")
        sum2_done = sem("sum2_done")
        pre_step = sem("pre_step")
        pre_done = sem("pre_done")
        tanh_done = sem("tanh_done")
        out_step = sem("out_step")
        eo_done = sem("eo_done")
        eo_kept = [sem(f"eo_kept{n}") for n in range(2)]
        far_done = sem("far_done")
        oh_done = sem("oh_done")
        node_done = sem("node_done")
        acc_done = sem("acc_done")
        fb_loaded = sem("fb_loaded")
        fb_step = sem("fb_step")
        fb_turn = sem("fb_turn")
        fb_oh = sem("fb_oh")
        fb_mm = sem("fb_mm")
        sums_ready = sem("sums_ready")
        nodes_turned = sem("nodes_turned")
        ln_step = sem("ln_step")
        var_ready = sem("var_ready")
        std_ready = sem("std_ready")
        y_ready = sem("y_ready")
        stored = sem("stored")

        block = ctx.enter_context(nc.Block())

        HEAD = 5
        TURNS = (NB - 2 - HEAD) // RING

        def steps(eng, step, lead):
            for c in range(HEAD):
                step(Block(0, c))
            with eng.Fori(0, TURNS) as turn:
                for c in range(HEAD, HEAD + RING):
                    step(Block(turn, c))
            for c in range(HEAD + RING * TURNS, NB + lead):
                step(Block(0, c))

        @block.sync
        def _(sp):
            sp.dma_start(vec_b[:], vec.rearrange("(b e) k -> b e k", b=NB)).then_inc(edges_loaded, 16)
            sp.dma_start(dst_b[:], dst.rearrange("(b e) -> b e", b=NB)).then_inc(edges_loaded, 16)
            sp.dma_start(wgt_b[:], weight.rearrange("(b e) -> b e", b=NB)).then_inc(edges_loaded, 16)

            def load(b):
                n = b.c % RING
                if b.known >= RING:
                    sp.wait_ge(gathered[n], b.turns(2 * T * 16))
                at = b.times(BE)
                sp.dma_start(src_r[n][:], src[bass.ds(at, BE)].rearrange("(p t) -> p t", t=T)).then_inc(idx_loaded[n], 16)
                sp.dma_start(dst_r[n][:], dst[bass.ds(at, BE)].rearrange("(p t) -> p t", t=T)).then_inc(idx_loaded[n], 16)
                if b.known >= RING:
                    sp.wait_ge(embt_done, b.times(1, 1 - RING))
                sp.dma_start(emb_r[n][:], emb[bass.ds(at, BE), :].rearrange("(p t) k -> p (t k)", t=T)).then_inc(emb_loaded[n], 16)

            def load_geo(b):
                n = b.c % RING
                if b.known >= RING:
                    sp.wait_ge(eo_done, b.times(1, 1 - RING))
                    sp.wait_ge(far_done, b.times(1, 1 - RING))
                sp.dma_start(geo_r[n][:], geo_dram[bass.ds(b.times(BE), BE), :].rearrange("(p t) k -> p t k", t=T)).then_inc(geo_loaded[n], 16)

            def keep(b):
                sp.wait_ge(eo_done, b.times(1, 1))
                sp.dma_start(eo_all[:, bass.ds(b.times(1), 1), :], eo_r[b.c % 2][:].rearrange("p t d -> p (t d)").unsqueeze(1)).then_inc(eo_kept[b.c % 2], 16)

            for c in range(RING):
                load(Block(0, c))
            sp.wait_ge(zeroed, 1)
            for t in range(T):
                for n, w in enumerate((w11, w21)):
                    sp.dma_start(w1bd[10 * t:10 * t + 10, t, n, :], w).then_inc(consts_loaded, 16)
            for n in range(S):
                rows = slice(J * n, J * n + J)
                for to, of, cols in ((0, 128, 128), (128, 0, 128), (256, 256, 256)):
                    sp.dma_start(w2f[rows, to:to + cols], w12[:, of:of + cols]).then_inc(consts_loaded, 16)
                for to, of, cols in ((0, 64, 64), (64, 192, 64), (128, 0, 64), (192, 128, 64), (256, 256, 128)):
                    sp.dma_start(w2f[rows, C1 + to:C1 + to + cols], w22[:, of:of + cols]).then_inc(consts_loaded, 16)
            sp.dma_start(bases[:], dst.rearrange("(b e) -> e b", b=NB)[0:1, :],
                         allow_slow_non_contiguous=True).then_inc(consts_loaded, 16)
            sp.dma_start(xn[:], x.rearrange("(p m) d -> p m d", p=P)).then_inc(nodes_loaded, 16)
            sp.wait_ge(geo_ready, 1)
            sp.dma_start(geo_dram.rearrange("(b e) k -> b e k", b=NB), geo_b[:]).then_inc(geo_stored, 16)
            sp.wait_ge(geo_stored, 16)
            for c in range(RING):
                load_geo(Block(0, c))
            load(Block(0, RING))
            load(Block(0, RING + 1))

            def step(b):
                if (b + 6).real:
                    load(b + 6)
                if (b + RING).real:
                    load_geo(b + RING)
                if b.real:
                    keep(b)

            for c in range(3):
                step(Block(0, c))
            turns = (NB - 6 - 3) // RING
            with sp.Fori(0, turns) as turn:
                for c in range(3, 3 + RING):
                    step(Block(turn, c))
            for c in range(3 + RING * turns, NB):
                step(Block(0, c))

            sp.wait_ge(misfits_ready, 1)
            flag = sp.value_load(misfits[0:1, 0:1], min_val=0, max_val=2 * NB)
            with sp.If(flag):
                sp.dma_start(dst_all[:], dst.rearrange("(b p t) -> p b t", p=P, t=T)).then_inc(fb_loaded, 16)
            with sp.Else():
                sp.nop()
            sp.wait_ge(y_ready, 1)
            sp.dma_start(out.rearrange("(p m) d -> p m d", p=P), yn[:]).then_inc(stored, 16)
            sp.wait_ge(stored, 16)
            for n in range(2):
                sp.wait_ge(eo_kept[n], 16 * len(range(n, NB, 2)))

        @block.gpsimd
        def _(pool):
            nc.gpsimd.memset(w1bd[:].rearrange("r t n j -> r (t n j)"), 0.0).then_inc(zeroed, 1)
            nc.gpsimd.memset(ones[:], 1.0).then_inc(pool_consts, 1)
            nc.gpsimd.iota(iota_i[:], pattern=[[1, P]], base=0, channel_multiplier=0).then_inc(pool_consts, 1)
            nc.gpsimd.memset(ident[:], 0.0).then_inc(pool_consts, 1)
            pool.wait_ge(pool_consts, 3)
            nc.gpsimd.affine_select(out=ident[:], in_=ident[:], compare_op=ALU.not_equal, fill=1.0, base=0,
                                    pattern=[[-1, 128]], channel_multiplier=1).then_inc(pool_consts, 1)

            def step(b):
                n = b.c % RING
                if not b.real:
                    return
                pool.wait_ge(idx_loaded[n], b.turns(32, 32))
                if b.known >= RING:
                    pool.wait_ge(f1_copied, b.times(5, 5 - 5 * RING))
                pool.sem_inc(gather_turn, 1)
                for t in range(T):
                    for k, idx in enumerate((src_r[n], dst_r[n])):
                        nc.gpsimd.indirect_dma_start(
                            x_r[n][:, t, k, :], None, x, bass.IndirectOffsetOnAxis(idx[:, t:t + 1], axis=0)
                        ).then_inc(gathered[n], 16)

            steps(pool, step, 0)

        @block.scalar
        def _(act):
            act.wait_ge(setup_step, 2)
            nc.scalar.activation(nrm_b[:], n2_b[:], ACT.Sqrt).then_inc(norm_ready, 1)

            def f1_copies(b):
                n, f1 = b.c % RING, f1_r[b.c % 2]
                act.wait_ge(gathered[n], b.turns(2 * T * 16, 2 * T * 16))
                if b.known >= 2:
                    act.wait_ge(p1_done, b.times(2 * NG, -2 * NG))
                xs = x_r[n][:]
                for k, of in ((1, xs[:, :, :, 0:8]), (2, xs[:, :, :, 0:8])) + tuple(
                        (3 + k, xs[:, :, :, 8 + k:D:3]) for k in range(3)):
                    nc.scalar.copy(f1[:, :, k, :].rearrange("p t (h u) -> p t h u", h=2), of).then_inc(f1_copied, 1)

            def one_hot(b):
                n = b.c % RING
                act.wait_ge(geo_loaded[n], b.turns(16, 16))
                if b.known >= 1:
                    act.wait_ge(oh_done, b.times(1))
                for t in range(T):
                    last = nc.scalar.activation(far[:, t, :], iota[:, 0:WIN], ACT.Abs, bias=geo_r[n][:, t, 3:4])
                last.then_inc(far_done, 1)
                act.wait_ge(far_done, b.times(1, 1))
                if b.known >= 2:
                    act.wait_ge(node_done, b.times(1, -1))
                nc.scalar.activation(oh_r[b.c % 2][:], far[:], ACT.Relu, scale=-1.0, bias=ones[:]).then_inc(oh_done, 1)

            def tanhs(b):
                if b.known >= 2:
                    act.wait_ge(eo_done, b.times(1, -1))
                act.wait_ge(pre_done, b.times(1, 1))
                nc.scalar.activation(th_r[b.c % 2][:], pre_r[b.c % 2][:], ACT.Tanh).then_inc(tanh_done, 1)

            def hidden(b):
                act.wait_ge(h_done, b.times(1, 1))
                if b.known >= 2:
                    act.wait_ge(part_ready[2], b.times(1, -1))
                nc.scalar.activation(h_r[b.c % 2][:].rearrange("p t n j -> p (t n j)"), h_ps, ACT.Relu,
                                     scale=1.0 / math.sqrt(10.0)).then_inc(h_ready, 1)

            def h_part(b, part):
                slots = [n for n, (k, _) in enumerate(SLOTS) if k == part]
                if part == 0:
                    act.wait_ge(h_ready, b.times(1, 1))
                    if b.known >= 2:
                        act.wait_ge(ht_done[1], b.times(1, -1))
                else:
                    act.wait_ge(rest_ready, b.times(2, part))
                hp, h = hp_r[b.c % 2], h_r[b.c % 2]
                for k in range(2):
                    last = nc.scalar.copy(hp[:, k, :, slots[0]:slots[-1] + 1, :],
                                          h[:, :, k, :].unsqueeze(2).to_broadcast([P, T, len(slots), J]))
                last.then_inc(part_ready[part], 1)

            def ht_copy(b, k):
                if b.known >= 2:
                    act.wait_ge((w1_done, w2_done)[k], b.times(NG, -NG))
                act.wait_ge(ht_done[k], b.times(1, 1))
                nc.scalar.copy(ht_r[k][b.c % 2][:].rearrange("r (t e) -> r t e", t=T), ht_ps).then_inc(ht_copied[k], 1)

            def embt_copy(b):
                if b.known >= 2:
                    act.wait_ge(h_done, b.times(1, -1))
                act.wait_ge(embt_done, b.times(1, 1))
                nc.scalar.copy(embt_r[b.c % 2][:], embt_ps).then_inc(embt_copied, 1)

            def step(b):
                if (b + 2).real:
                    embt_copy(b + 2)
                if (b + 1).real:
                    f1_copies(b + 1)
                    ht_copy(b + 1, 0)
                if (b + 2).real:
                    hidden(b + 2)
                    h_part(b + 2, 0)
                if (b + -2).real:
                    one_hot(b + -2)
                    tanhs(b + -2)
                if (b + 1).real:
                    ht_copy(b + 1, 1)
                if (b + 2).real:
                    h_part(b + 2, 1)
                    h_part(b + 2, 2)

            act.wait_ge(consts_ready, 3)
            step(Block(0, -2))
            step(Block(0, -1))
            steps(act, step, 3)
            act.wait_ge(var_ready, 1)
            nc.scalar.activation(st[:, 2, :], st[:, 1, :], ACT.Sqrt).then_inc(std_ready, 1)

        @block.vector
        def _(dve):
            setup = [0]

            def link(ins):
                setup[0] += 1
                ins.then_inc(setup_step, 1)
                dve.wait_ge(setup_step, setup[0])

            dve.wait_ge(edges_loaded, 48)
            link(nc.vector.tensor_tensor(geo_b[:, :, 0:3], vec_b[:], vec_b[:], ALU.mult))
            link(nc.vector.tensor_reduce(n2_b[:], geo_b[:, :, 0:3], AX.X, ALU.add))
            nc.vector.memset(acc[:], 0.0)
            link(nc.vector.tensor_copy(dstf_b[:], dst_b[:]))
            link(nc.vector.tensor_scalar(geo_b[:, :, 3], dstf_b[:], -1.0, dstf_b[:, 0:1], ALU.mult, ALU.add))
            link(nc.vector.tensor_copy(geo_b[:, :, 4], wgt_b[:]))
            dve.wait_ge(norm_ready, 1)
            link(nc.vector.reciprocal(inv_b[:], nrm_b[:]))
            link(nc.vector.tensor_tensor(dstf_b[:], n2_b[:], inv_b[:], ALU.mult))
            link(nc.vector.tensor_tensor(dstf_b[:], dstf_b[:], inv_b[:], ALU.mult))
            link(nc.vector.tensor_scalar(dstf_b[:], dstf_b[:], -0.5, 1.5, ALU.mult, ALU.add))
            link(nc.vector.tensor_tensor(inv_b[:], inv_b[:], dstf_b[:], ALU.mult))
            nc.vector.tensor_tensor(geo_b[:, :, 0:3], vec_b[:], inv_b[:].unsqueeze(2).to_broadcast([NB, BE, 3]),
                                    ALU.mult).then_inc(geo_ready, 1)
            dve.wait_ge(pool_consts, 4)
            nc.vector.tensor_copy(iota[:], iota_i[:]).then_inc(consts_ready, 1)
            nc.vector.tensor_copy(ident_h[:], ident[0:P, 0:P]).then_inc(consts_ready, 1)
            dve.wait_ge(consts_loaded, 16 * (2 * T + 8 * S + 1))
            c1, c2 = 0.25 / math.sqrt(32.0), 1.0 / 16.0
            for a, b, c in ((0, 256, c1), (256, 384, c1 * SQRT3), (384, C1, c1),
                            (C1, C1 + 256, c2), (C1 + 256, C1 + 320, c2 * SQRT3), (C1 + 320, C1 + C2, c2)):
                link(nc.vector.tensor_scalar(w2f[:, a:b], w2f[:, a:b], c, None, ALU.mult))
            for n in range(3):
                link(nc.vector.tensor_copy(w2part[n][:], w2f[:]))
                if n < 2:
                    link(nc.vector.tensor_tensor(w2f[:], w2f[:], w2part[n][:], ALU.subtract))
            rows = ident[0:S * J, 0:S * J].rearrange("p (s j) -> p s j", s=S)
            for n, (a, b, c) in enumerate(((0, 4, 3), (1, 5, 3), (2, 3, 1), (5, 6, 1))):
                link(nc.vector.tensor_reduce(slot_mask[:, n:n + 1], rows[:, a:b:c, :], AX.XY, ALU.add))
            link(nc.vector.tensor_tensor(slot_mask[:, 0:1], slot_mask[:, 0:1], slot_mask[:, 3:4], ALU.add))
            link(nc.vector.tensor_scalar(w2s[:], w2part[0][:], slot_mask[:, 0:1], None, ALU.mult))
            for n in (1, 2):
                last = nc.vector.scalar_tensor_tensor(out=w2s[:], in0=w2part[n][:], scalar=slot_mask[:, n:n + 1],
                                                      in1=w2s[:], op0=ALU.mult, op1=ALU.add)
                if n == 1:
                    link(last)
            last.then_inc(consts_ready, 1)
            link(nc.vector.tensor_reduce(ext[:, 0:1], geo_b[:, :, 3], AX.X, ALU.max))
            link(nc.vector.tensor_reduce(ext[:, 1:2], geo_b[:, :, 3], AX.X, ALU.min))
            link(nc.vector.tensor_scalar(ext[:, 0:1], ext[:, 0:1], 0.0, None, ALU.is_gt))
            link(nc.vector.tensor_scalar(ext[:, 1:2], ext[:, 1:2], 1.0 - WIN, None, ALU.is_lt))
            nc.vector.tensor_tensor(ext[:, 2:3], ext[:, 0:1], ext[:, 1:2], ALU.add).then_inc(misfit_parts, 1)
            dve.wait_ge(misfit_sum, 1)
            nc.vector.tensor_copy(misfits[:], ps[0:1, 0, 0:1]).then_inc(misfits_ready, 1)

            def directions(b, v):
                return geo_r[b.c % RING][:, :, 0:3].unsqueeze(3).to_broadcast([P, T, 3, v])

            def f1_make(b):
                n, f1 = b.c % RING, f1_r[b.c % 2]
                dve.wait_ge(geo_loaded[n], b.turns(16, 16))
                dve.wait_ge(f1_copied, b.times(5, 5))
                nc.vector.tensor_tensor(tmp1[:], f1[:, :, 3:6, :], directions(b, V1), ALU.mult).then_inc(f1_scratch, 1)
                dve.wait_ge(f1_scratch, b.times(1, 1))
                nc.vector.tensor_reduce(f1[:, :, 0, :], tmp1[:].rearrange("p t k u -> p t u k"), AX.X,
                                        ALU.add).then_inc(f1_made, 1)

            def f2_make(b):
                f2, dirs = f2_r[b.c % 2], directions(b, W)
                dve.wait_ge(sum1_done, b.times(1, 1))
                nc.vector.tensor_copy(tmp5[:], sum1[:, :, 0, :]).then_inc(f2_step, 1)
                nc.vector.tensor_tensor(tmp2[:], sum1[:, :, 2:3, :].to_broadcast([P, T, 3, W]), dirs,
                                        ALU.mult).then_inc(f2_step, 1)
                dve.wait_ge(f2_step, b.times(7, 2))
                nc.vector.tensor_tensor(f2[:, :, 5:8, :], tmp2[:], sum1[:, :, 3:6, :], ALU.add).then_inc(f2_step, 1)
                nc.vector.tensor_tensor(f2[:, :, 2:5, :], tmp5[:].unsqueeze(2).to_broadcast([P, T, 3, W]),
                                        sum1[:, :, 1:2, :].to_broadcast([P, T, 3, W]), ALU.add).then_inc(f2_step, 1)
                dve.wait_ge(f2_step, b.times(7, 4))
                nc.vector.tensor_tensor(tmp3[:], f2[:, :, 5:8, :], dirs, ALU.mult).then_inc(f2_step, 1)
                dve.wait_ge(f2_step, b.times(7, 5))
                for k in range(2):
                    nc.vector.tensor_reduce(f2[:, :, k, :], tmp3[:].rearrange("p t k u -> p t u k"), AX.X,
                                            ALU.add).then_inc(f2_step, 1)

            def times(wps, f, p):
                _, t, k, u, w = p.shape
                k_w = wps.shape[2]
                if k_w == k:
                    return nc.vector.tensor_tensor(p.rearrange("p t k u w -> p t (k u) w"),
                                                   wps.rearrange("p t k (u w) -> p t (k u) w", w=w),
                                                   f.rearrange("p t k u -> p t (k u)").unsqueeze(3).to_broadcast([P, t, k * u, w]),
                                                   ALU.mult)
                return nc.vector.tensor_tensor(p, wps.rearrange("p t k (u w) -> p t k u w", w=w).to_broadcast([P, t, k, u, w]),
                                               f.unsqueeze(4).to_broadcast([P, t, k, u, w]), ALU.mult)

            def products1(b, first, end):
                f1, p1 = f1_r[b.c % 2], p1_r[b.c % 2]
                dve.wait_ge(f1_made, b.times(1, 1))
                if b.known >= 2 and first == 0:
                    dve.wait_ge(sum1_done, b.times(1, -1))
                for n in range(first, end):
                    t, tiles, bank = GROUPS[0][n]
                    wps = ps[0:P, bank:bank + tiles, :].rearrange("p t (g v) -> p t g v", g=4)
                    dve.wait_ge(w1_done, b.times(NG, n + 1))
                    times(wps[:, :, 0:3], f1[:, t:t + tiles, 0:3], p1[:, t:t + tiles, 0:3]).then_inc(p1_done, 1)
                    times(wps[:, :, 3:4], f1[:, t:t + tiles, 3:6], p1[:, t:t + tiles, 3:6]).then_inc(p1_done, 1)

            def halve1(b):
                p1 = p1_r[b.c % 2]
                dve.wait_ge(p1_done, b.times(2 * NG, 2 * NG))
                lo, hi = (p1[:, :, :, a:a + HALF1, :].rearrange("p t k u w -> p (t k) (u w)") for a in (0, V1 - HALF1))
                nc.vector.tensor_tensor(lo, lo, hi, ALU.add).then_inc(half1_done, 1)

            def products2(b):
                f2, p2 = f2_r[b.c % 2], p2_r[b.c % 2]
                dve.wait_ge(f2_step, b.times(7, 7))
                if b.known >= 2:
                    dve.wait_ge(sum2_done, b.times(1, -1))
                for n, (t, tiles, bank) in enumerate(GROUPS[1]):
                    wps = ps[0:P, bank:bank + tiles, 0:C2].rearrange("p t (g v) -> p t g v", g=6)
                    dve.wait_ge(w2_done, b.times(NG, n + 1))
                    times(wps[:, :, 0:5], f2[:, t:t + tiles, 0:5], p2[:, t:t + tiles, 0:5]).then_inc(p2_done, 1)
                    times(wps[:, :, 5:6], f2[:, t:t + tiles, 5:8], p2[:, t:t + tiles, 5:8]).then_inc(p2_done, 1)

            def h_rest(b, part):
                dve.wait_ge(part_ready[part], b.times(1, 1))
                slot = [n for n, (k, _) in enumerate(SLOTS) if k == part][0]
                h = h_r[b.c % 2][:]
                nc.vector.tensor_tensor(h, h, hp_r[b.c % 2][:, :, :, slot, :].rearrange("p k t j -> p t k j"),
                                        ALU.subtract).then_inc(rest_ready, 1)

            def pre_output(b):
                dve.wait_ge(sum2_done, b.times(1, 1))
                pre = pre_r[b.c % 2]
                nc.vector.tensor_copy(pre[:], sum2[:, :, 0:2, :]).then_inc(pre_step, 1)
                nc.vector.tensor_tensor(tmp4[:], sum2[:, :, 4:5, :].to_broadcast([P, T, 3, W]), directions(b, W),
                                        ALU.mult).then_inc(pre_step, 1)
                dve.wait_ge(pre_step, b.times(2, 2))
                nc.vector.tensor_tensor(pre[:], pre[:], sum2[:, :, 2:4, :], ALU.add).then_inc(pre_done, 1)
                nc.vector.tensor_tensor(tmp4[:], tmp4[:], sum2[:, :, 5:8, :], ALU.add).then_inc(out_step, 1)

            def output(b):
                th, eo, geo = th_r[b.c % 2], eo_r[b.c % 2], geo_r[b.c % RING]
                wb = geo[:, :, 4:5].to_broadcast([P, T, W])
                dve.wait_ge(tanh_done, b.times(1, 1))
                nc.vector.tensor_tensor(gate[:], th[:, :, 1, :], wb, ALU.mult).then_inc(out_step, 1)
                if b.known >= 2:
                    dve.wait_ge(node_done, b.times(1, -1))
                    dve.wait_ge(eo_kept[b.c % 2], b.pairs(16))
                nc.vector.tensor_tensor(eo[:, :, 0:8], th[:, :, 0, :], wb, ALU.mult).then_inc(out_step, 1)
                dve.wait_ge(out_step, b.times(3, 3))
                nc.vector.tensor_tensor(eo[:, :, 8:D].rearrange("p t (u k) -> p t k u", k=3), tmp4[:],
                                        gate[:].unsqueeze(2).to_broadcast([P, T, 3, W]), ALU.mult).then_inc(eo_done, 1)

            def accumulate(b):
                base = dve.value_load(bases[0:1, bass.ds(b.times(1), 1)], min_val=0, max_val=N - 1)
                dve.wait_ge(node_done, b.times(1, 1))
                if b.known >= 1:
                    dve.wait_ge(acc_done, b.times(1))
                nodes = acc[:, bass.ds(base, WIN)]
                nc.vector.tensor_tensor(nodes, nodes, node_ps, ALU.add).then_inc(acc_done, 1)

            def step(b):
                if b.real:
                    products1(b, 0, 2)
                if (b + -3).real:
                    accumulate(b + -3)
                if b.real:
                    products1(b, 2, NG)
                    halve1(b)
                if (b + -1).real:
                    f2_make(b + -1)
                if (b + 1).real:
                    f1_make(b + 1)
                if (b + 2).real:
                    h_rest(b + 2, 0)
                if (b + -2).real:
                    pre_output(b + -2)
                if (b + -1).real:
                    products2(b + -1)
                if (b + 2).real:
                    h_rest(b + 2, 1)
                if (b + -2).real:
                    output(b + -2)

            step(Block(0, -2))
            step(Block(0, -1))
            steps(dve, step, 3)

            flag = dve.value_load(misfits[0:1, 0:1], min_val=0, max_val=2 * NB)
            with dve.If(flag):
                dve.wait_ge(fb_loaded, 16)
                dve.wait_ge(acc_done, NB)
                nc.vector.memset(acc[:], 0.0).then_inc(fb_step, 1)
                dve.wait_ge(fb_step, 1)
                with dve.Fori(0, NB) as i:
                    nc.vector.tensor_copy(dst_w[:], dst_all[:, bass.ds(i, 1), :].rearrange("p b t -> p (b t)")).then_inc(fb_step, 1)
                    nc.vector.tensor_copy(eo_s[:].rearrange("p t d -> p (t d)"),
                                          eo_all[:, bass.ds(i, 1), :].rearrange("p b n -> p (b n)")).then_inc(fb_step, 1)
                    dve.wait_ge(fb_step, i * (2 + 2 * NT) + 3)
                    dve.sem_inc(fb_turn, 1)
                    with dve.Fori(0, NT) as m:
                        nc.vector.tensor_tensor(oh_w[:], iota[:].unsqueeze(1).to_broadcast([P, T, P]),
                                                dst_w[:].unsqueeze(2).to_broadcast([P, T, P]), ALU.is_equal).then_inc(fb_oh, 1)
                        dve.wait_ge(fb_oh, i * NT + m + 1)
                        nc.vector.tensor_scalar(dst_w[:], dst_w[:], -float(P), None, ALU.add).then_inc(fb_step, 1)
                        dve.wait_ge(fb_mm, i * NT + m + 1)
                        nodes = acc[:, bass.ds(m * P, P)]
                        nc.vector.tensor_tensor(nodes, nodes, ps[0:D, 0, 0:P], ALU.add).then_inc(fb_step, 1)
                        dve.wait_ge(fb_step, i * (2 + 2 * NT) + m * 2 + 5)
                nc.vector.engine_nop().then_inc(sums_ready, 1)
            with dve.Else():
                dve.wait_ge(acc_done, NB)
                nc.vector.engine_nop().then_inc(sums_ready, 1)

            turned = [0]

            def chain(ins):
                turned[0] += 1
                ins.then_inc(ln_step, 1)
                dve.wait_ge(ln_step, turned[0])

            def wide(a):
                return a.unsqueeze(2).to_broadcast([P, NT, D])

            dve.wait_ge(nodes_loaded, 16)
            dve.wait_ge(nodes_turned, 1)
            chain(nc.vector.tensor_tensor(yn[:].rearrange("p m d -> p (m d)"), xn[:].rearrange("p m d -> p (m d)"),
                                          ps[0:P].rearrange("p b c -> p (b c)")[:, 0:NT * D], ALU.add))
            chain(nc.vector.tensor_reduce(st[:, 0, :], yn[:], AX.X, ALU.add))
            chain(nc.vector.tensor_scalar(st[:, 0, :], st[:, 0, :], 1.0 / D, None, ALU.mult))
            chain(nc.vector.tensor_tensor(yn[:], yn[:], wide(st[:, 0, :]), ALU.subtract))
            chain(nc.vector.tensor_tensor(xn[:], yn[:], yn[:], ALU.mult))
            chain(nc.vector.tensor_reduce(st[:, 5, :], xn[:], AX.X, ALU.add))
            nc.vector.tensor_scalar(st[:, 1, :], st[:, 5, :], 1.0 / D, EPS, ALU.mult, ALU.add).then_inc(var_ready, 1)
            dve.wait_ge(std_ready, 1)
            chain(nc.vector.reciprocal(st[:, 3, :], st[:, 2, :]))
            chain(nc.vector.tensor_tensor(st[:, 4, :], st[:, 3, :], st[:, 1, :], ALU.mult))
            chain(nc.vector.tensor_tensor(st[:, 4, :], st[:, 4, :], st[:, 3, :], ALU.mult))
            chain(nc.vector.tensor_scalar(st[:, 4, :], st[:, 4, :], -0.5, 1.5, ALU.mult, ALU.add))
            chain(nc.vector.tensor_tensor(st[:, 3, :], st[:, 3, :], st[:, 4, :], ALU.mult))
            nc.vector.tensor_tensor(yn[:], yn[:], wide(st[:, 3, :]), ALU.mult).then_inc(y_ready, 1)

        @block.tensor
        def _(pe):
            idn = ident[0:P, 0:P]
            pe.wait_ge(pool_consts, 4)
            pe.wait_ge(misfit_parts, 1)
            nc.tensor.matmul(ps[0:1, 0, 0:1], ext[:, 2:3], ones[0:NB, :], start=True, stop=True).then_inc(misfit_sum, 1)
            pe.wait_ge(misfits_ready, 1)
            pe.wait_ge(consts_ready, 3)

            def ht(b, k):
                pe.wait_ge(part_ready[2], b.times(1, 1))
                if k == 1:
                    pe.wait_ge(ht_copied[0], b.times(1, 1))
                elif b.known >= 1:
                    pe.wait_ge(ht_copied[1], b.times(1))
                if k == 0 and b.known >= 4:
                    pe.wait_ge(acc_done, b.times(1, -3))
                for t in range(T):
                    last = nc.tensor.transpose(ht_ps[:, t, :],
                                               hp_r[b.c % 2][:, k, t].rearrange("p s j -> p (s j)"), ident_h[:])
                last.then_inc(ht_done[k], 1)

            def w(b, k, n):
                if n == 0:
                    pe.wait_ge(ht_copied[k], b.times(1, 1))
                if k == 0 and n < 2 and b.known == 1:
                    pe.wait_ge(p1_done, 2 * NG)
                if n == 2:
                    pe.wait_ge((p1_done, p2_done)[k], b.times(2 * NG, 2))
                elif k == 0 and b.known >= 2:
                    pe.wait_ge(p2_done, b.times(2 * NG, 2 * (n + 2 - 2 * NG)))
                elif k == 1 and n == 0:
                    pe.wait_ge(p1_done, min_block(b + 1, 2 * NG, 4))
                elif k == 1:
                    pe.wait_ge(p1_done, min_block(b + 1, 2 * NG, 6))
                t, tiles, bank = GROUPS[k][n]
                cols = slice(0, C1) if k == 0 else slice(C1, C1 + C2)
                for i in range(tiles):
                    last = nc.tensor.matmul(ps[0:P, bank + i, 0:cols.stop - cols.start],
                                            ht_r[k][b.c % 2][:, P * (t + i):P * (t + i) + P], w2s[:, cols],
                                            start=True, stop=True)
                last.then_inc((w1_done, w2_done)[k], 1)

            def min_block(b, k, plus):
                return k * NB if isinstance(b.turn, int) and b.c >= NB else b.times(k, plus)

            def sums(u, left, p, dest):
                return nc.tensor.matmul(dest, idn, p[:, :, :, u, :], start=(u == 0), stop=(u == left - 1))

            def sum_1(b, u):
                left = V1 - HALF1
                if u == 0:
                    pe.wait_ge(half1_done, b.times(1, 1))
                    if b.known >= 1:
                        pe.wait_ge(f2_step, b.times(7, -3))
                last = sums(u, left, p1_r[b.c % 2], sum1)
                if u == left - 1:
                    last.then_inc(sum1_done, 1)

            def sum_2(b, u):
                if u == 0:
                    pe.wait_ge(p2_done, b.times(2 * NG, 2 * NG))
                    if b.known >= 1:
                        pe.wait_ge(out_step, b.times(3, -2))
                last = sums(u, V2, p2_r[b.c % 2], sum2)
                if u == V2 - 1:
                    last.then_inc(sum2_done, 1)

            def over_nodes(b):
                pe.wait_ge(oh_done, b.times(1, 1))
                pe.wait_ge(ht_copied[1], min_block(b + 3, 1, 1))
                pe.wait_ge(eo_done, b.times(1, 1))
                for t in range(T):
                    last = nc.tensor.matmul(node_ps, eo_r[b.c % 2][:, t, :], oh_r[b.c % 2][:, t, :],
                                            start=(t == 0), stop=(t == T - 1))
                last.then_inc(node_done, 1)

            def embt(b):
                n = b.c % RING
                pe.wait_ge(emb_loaded[n], b.turns(16, 16))
                if b.known >= 1:
                    pe.wait_ge(h_ready, b.times(1))
                nc.tensor.matmul(embt_ps, emb_r[n][:], idn, start=True, stop=True).then_inc(embt_done, 1)

            def first_layer(b):
                pe.wait_ge(embt_copied, b.times(1, 1))
                nc.tensor.matmul(h_ps, embt_r[b.c % 2][:], w1bd[:].rearrange("r t n j -> r (t n j)"),
                                 start=True, stop=True).then_inc(h_done, 1)

            def step(b):
                def part(which, lo, hi):
                    if which == 1 and b.real:
                        for u in range(lo, hi):
                            sum_1(b, u)
                    if which == 2 and (b + -2).real:
                        for u in range(lo, hi):
                            sum_2(b + -2, u)

                if (b + 2).real:
                    embt(b + 2)
                if (b + -3).real:
                    over_nodes(b + -3)
                part(2, 0, 2)
                if b.real:
                    w(b, 0, 2)
                part(2, 2, 4)
                if (b + 2).real:
                    first_layer(b + 2)
                if (b + -1).real:
                    w(b + -1, 1, 0)
                part(2, 4, 6)
                if (b + 1).real:
                    ht(b + 1, 0)
                part(2, 6, 8)
                if (b + -1).real:
                    w(b + -1, 1, 1)
                part(1, 0, 4)
                if (b + -1).real:
                    w(b + -1, 1, 2)
                if (b + 1).real:
                    ht(b + 1, 1)
                part(1, 4, 7)
                if (b + 1).real:
                    w(b + 1, 0, 0)
                part(1, 7, 9)
                if (b + 1).real:
                    w(b + 1, 0, 1)
                part(1, 9, V1 - HALF1)

            step(Block(0, -2))
            step(Block(0, -1))
            steps(pe, step, 3)

            flag = pe.value_load(misfits[0:1, 0:1], min_val=0, max_val=2 * NB)
            with pe.If(flag):
                with pe.Fori(0, NB) as i:
                    with pe.Fori(0, NT) as m:
                        pe.wait_ge(fb_oh, i * NT + m + 1)
                        for t in range(T):
                            last = nc.tensor.matmul(ps[0:D, 0, 0:P], eo_s[:, t, :], oh_w[:, t, :],
                                                    start=(t == 0), stop=(t == T - 1))
                        last.then_inc(fb_mm, 1)
            with pe.Else():
                pe.nop()
            pe.wait_ge(sums_ready, 1)
            for m in range(NT):
                b, at = divmod(m * D, 512)
                last = nc.tensor.transpose(ps[0:P, b, at:at + D], acc[:, m:N:NT], ident[0:D, 0:D])
            last.then_inc(nodes_turned, 1)


def kernel(x, src, dst, edge_attr_10, edge_attr_3, edge_weight,
           L0_gnn_fc1_w1, L0_gnn_fc1_w2, L0_gnn_fc2_w1, L0_gnn_fc2_w2):
    import numpy as np
    import concourse.bacc as bacc
    from concourse.bass_utils import run_bass_kernel_spmd

    nc = bacc.Bacc("TRN2", target_bir_lowering=False, num_devices=1)
    given = {"x": x, "src": src, "dst": dst, "emb": edge_attr_10, "vec": edge_attr_3, "weight": edge_weight,
             "w11": L0_gnn_fc1_w1, "w12": L0_gnn_fc1_w2, "w21": L0_gnn_fc2_w1, "w22": L0_gnn_fc2_w2}
    arrays, args = {}, {}
    for name, a in given.items():
        a = np.ascontiguousarray(a)
        arrays[f"in_{name}"] = a
        args[name] = nc.dram_tensor(f"in_{name}", a.shape, mybir.dt.from_np(a.dtype), kind="ExternalInput").ap()
    args["out"] = nc.dram_tensor("out_y", (N, D), F32, kind="ExternalOutput").ap()
    program(nc, **args)
    r = run_bass_kernel_spmd(nc, [arrays], core_ids=[0])
    return r.results[0]["out_y"]
```

```python
import math
from contextlib import ExitStack

import concourse.bass as bass
from concourse import mybir

F32 = mybir.dt.float32
BF16 = mybir.dt.bfloat16
I32 = mybir.dt.int32
ALU = mybir.AluOpType
ACT = mybir.ActivationFunctionType
AX = mybir.AxisListType

N = 3125
E = 53125
D = 32
P = 125
T = 5
BE = P * T
NB = E // BE
J = 16
W = 8
V1 = 16
V2 = 8
K1 = 6
K2 = 8
C1 = 4 * V1 * W
C2 = 6 * V2 * W
WIN = 64
HALF1 = 6
KS1 = K1 - 1
KS2 = K2 - 2
SLOTS = ((0, 0), (0, 1), (0, 2), (1, 0), (1, 1), (2, 0))
S = len(SLOTS)
NT = N // P
RING = 4
GROUPS = (((0, 2, 0), (2, 2, 2), (4, 1, 0)), ((0, 2, 2), (2, 2, 0), (4, 1, 2)))
NG = len(GROUPS[0])
SQRT3 = math.sqrt(3.0)
EPS = 1e-5


class Block:

    def __init__(self, turn, c):
        self.turn, self.c = turn, c

    def __add__(self, d):
        return Block(self.turn, self.c + d)

    def times(self, k, plus=0):
        if isinstance(self.turn, int):
            return k * (RING * self.turn + self.c) + plus
        return self.turn * (RING * k) + (k * self.c + plus)

    def turns(self, k, plus=0):
        return self.turn * k + (k * (self.c // RING) + plus)

    def pairs(self, k, plus=0):
        return self.turn * (RING // 2 * k) + (k * (self.c // 2) + plus)

    @property
    def known(self):
        return self.c if isinstance(self.turn, int) else min(max(self.c, RING), NB - RING)

    @property
    def real(self):
        return 0 <= self.c < NB or not isinstance(self.turn, int)


def program(nc, x, src, dst, emb, vec, weight, w11, w12, w21, w22, out):
    ctx = ExitStack()
    with ctx:
        def sb(name, shape, dt=F32):
            return ctx.enter_context(nc.sbuf_tensor(name, shape, dt))

        def sem(name):
            return ctx.enter_context(nc.semaphore(name))

        ident = sb("ident", [128, 128])
        iota_i = sb("iota_i", [P, P], I32)
        iota = sb("iota", [P, P])
        ones = sb("ones", [2 * WIN, 1])
        slot_mask = sb("slot_mask", [S * J, 4])
        w2f = sb("w2f", [S * J, C1 + C2])
        w2part = [sb(f"w2part{n}", [S * J, C1 + C2], BF16) for n in range(3)]
        w2s = sb("w2s", [S * J, C1 + C2], BF16)
        w1bd = sb("w1bd", [T * 10, T, 2, J])
        ident_h = sb("ident_h", [P, P], BF16)
        rank_i = sb("rank_i", [2 * WIN, 1], I32)
        rank_high = sb("rank_high", [2 * WIN, 1])
        rank = sb("rank", [2 * WIN, 1])
        no_rows = sb("no_rows", [WIN, 3, D], BF16)
        x_part = sb("x_part", [P, 3, NT, D], BF16)
        dst_b = sb("dst_b", [NB, BE], I32)
        dstf_b = sb("dstf_b", [NB, BE])
        wgt_b = sb("wgt_b", [NB, BE])
        n2_b = sb("n2_b", [NB, BE])
        nrm_b = sb("nrm_b", [NB, BE])
        inv_b = sb("inv_b", [NB, BE])
        place_b = sb("place_b", [NB, BE])
        ext = sb("ext", [NB, 4])
        misfits = sb("misfits", [1, 1], I32)
        bases = sb("bases", [1, NB], I32)
        geo_dram = nc.dram_tensor("geo_dram", (E, 5), F32, kind="Internal").ap()
        place_dram = nc.dram_tensor("place_dram", (E,), F32, kind="Internal").ap()
        x_dram = nc.dram_tensor("x_dram", (3, N + WIN, D), BF16, kind="Internal").ap()
        src_r = [sb(f"src{n}", [P, T], I32) for n in range(RING)]
        dst_r = [sb(f"dst{n}", [P, T], I32) for n in range(RING)]
        emb_r = [sb(f"emb{n}", [P, T * 10]) for n in range(RING)]
        geo_r = [sb(f"geo{n}", [P, T, 5]) for n in range(RING)]
        x_r = [sb(f"x{n}", [P, T, 2, D]) for n in range(RING)]
        h_r = [sb(f"h{n}", [P, T, 2, J]) for n in range(2)]
        hp_r = [sb(f"hp{n}", [P, 2, T, S, J], BF16) for n in range(2)]
        ht_r = [[sb(f"ht{k}_{n}", [S * J, T * P], BF16) for n in range(2)] for k in range(2)]
        f1_r = [sb(f"f1_{n}", [P, T, K1, V1]) for n in range(2)]
        f2_r = [sb(f"f2_{n}", [P, T, K2, V2]) for n in range(2)]
        embt_r = [sb(f"embt{n}", [T * 10, P]) for n in range(2)]
        p1_r = [sb(f"p1_{n}", [P, T, K1, V1, W]) for n in range(2)]
        p2_r = [sb(f"p2_{n}", [P, T, K2, V2, W]) for n in range(2)]
        vec_b = p2_r[1][0:NB].rearrange("p t k u w -> p (t k u w)")[:, 0:3 * BE].rearrange("p (e k) -> p e k", k=3)
        geo_b = p1_r[1][0:NB].rearrange("p t k u w -> p (t k u w)")[:, 0:5 * BE].rearrange("p (e k) -> p e k", k=5)
        th_r = [sb(f"th{n}", [P, T, 2, W]) for n in range(2)]
        eo_r = [sb(f"eo{n}", [P, T, W + D]) for n in range(2)]
        oh_r = [sb(f"oh{n}", [P, T, WIN]) for n in range(2)]
        far = sb("far", [P, T, WIN])
        place_r = [sb(f"place{n}", [2 * WIN, BE]) for n in range(2)]
        window_r = [sb(f"window{n}", [2 * WIN, 2, D], BF16) for n in range(2)]
        far_t = sb("far_t", [2 * WIN, T, P])
        oht_r = [sb(f"oht{n}", [2 * WIN, T, P], BF16) for n in range(2)]
        f1_products = sb("f1_products", [P, T, 3, V1])
        f1_pair = sb("f1_pair", [P, T, V1])
        sv_directed = sb("sv_directed", [P, T, 3, W])
        f2_products = sb("f2_products", [P, T, 3, W])
        vectors_r = [sb(f"vectors{n}", [P, T, 3, W]) for n in range(2)]
        acc = sb("acc", [D, N + WIN])
        eo_all = sb("eo_all", [P, NB, T * D])
        eo_s = sb("eo_s", [P, T, D])
        dst_all = sb("dst_all", [P, NB, T], I32)
        dst_w = sb("dst_w", [P, T])
        oh_w = sb("oh_w", [P, T, P])
        xn = sb("xn", [P, NT, D])
        yn = sb("yn", [P, NT, D])
        st = sb("st", [P, 6, NT])

        ps = ctx.enter_context(nc.psum_tensor("ps", [128, 8, 512], F32))
        embt_ps = ps[0:T * 10, 6, 0:P]
        h_ps = ps[0:P, 6, 128:128 + T * 2 * J]
        rows_ps = ps[0:P, 6, 288:288 + T * D].rearrange("p (t d) -> p t d", t=T)
        ht_ps = ps[0:S * J, 7, :].bitcast(BF16)[:, 0:T * (P + 1)].rearrange("r (t e) -> r t e", t=T)[:, :, 0:P]
        node_ps = ps[0:D, 7, 384:384 + WIN]
        sum1 = ps[0:P, 4, 0:T * KS1 * W].rearrange("p (t g w) -> p t g w", t=T, g=KS1)
        sum2 = ps[0:P, 5, 0:T * KS2 * W].rearrange("p (t g w) -> p t g w", t=T, g=KS2)

        w1_loaded = sem("w1_loaded")
        w2_loaded = sem("w2_loaded")
        bases_loaded = sem("bases_loaded")
        nodes_loaded = sem("nodes_loaded")
        vec_loaded = sem("vec_loaded")
        dst_loaded = sem("dst_loaded")
        weight_loaded = sem("weight_loaded")
        pool_consts = sem("pool_consts")
        zeroed = sem("zeroed")
        iota_ready = sem("iota_ready")
        ident_ready = sem("ident_ready")
        geo_copied = sem("geo_copied")
        w2_scaled = sem("w2_scaled")
        w2_part = sem("w2_part")
        w2_rest = sem("w2_rest")
        w2_ready = sem("w2_ready")
        setup_step = sem("setup_step")
        norm_ready = sem("norm_ready")
        geo_ready = sem("geo_ready")
        geo_stored = sem("geo_stored")
        misfit_parts = sem("misfit_parts")
        misfit_sum = sem("misfit_sum")
        misfits_ready = sem("misfits_ready")
        idx_loaded = [sem(f"idx_loaded{n}") for n in range(RING)]
        emb_loaded = [sem(f"emb_loaded{n}") for n in range(RING)]
        geo_loaded = [sem(f"geo_loaded{n}") for n in range(RING)]
        window_loaded = [sem(f"window_loaded{n}") for n in range(2)]
        place_ready = sem("place_ready")
        place_stored = sem("place_stored")
        x_part_ready = sem("x_part_ready")
        x_rest = sem("x_rest")
        x_stored = sem("x_stored")
        far_t_done = sem("far_t_done")
        oht_done = sem("oht_done")
        rows_done = sem("rows_done")
        rows_copied = sem("rows_copied")
        rows_final = [sem(f"rows_final{n}") for n in range(RING)]
        gathered = [sem(f"gathered{n}") for n in range(RING)]
        gather_turn = sem("gather_turn")
        embt_done = sem("embt_done")
        embt_copied = sem("embt_copied")
        h_done = sem("h_done")
        h_ready = sem("h_ready")
        part_ready = [sem(f"part_ready{n}") for n in range(3)]
        rest_ready = sem("rest_ready")
        ht_done = [sem(f"ht_done{n}") for n in range(2)]
        ht_copied = [sem(f"ht_copied{n}") for n in range(2)]
        f1_copied = sem("f1_copied")
        f1_step = sem("f1_step")
        f1_made = sem("f1_made")
        f2_copied = sem("f2_copied")
        f2_step = sem("f2_step")
        f2_twice = sem("f2_twice")
        w1_done = sem("w1_done")
        w2_done = sem("w2_done")
        p1_done = sem("p1_done")
        p2_done = sem("p2_done")
        fold1_done = sem("fold1_done")
        half1_done = sem("half1_done")
        fold2_done = sem("fold2_done")
        sum1_done = sem("sum1_done")
        sum2_done = sem("sum2_done")
        tanh_done = sem("tanh_done")
        vectors_step = sem("vectors_step")
        out_step = sem("out_step")
        eo_done = sem("eo_done")
        eo_kept = [sem(f"eo_kept{n}") for n in range(2)]
        far_done = sem("far_done")
        oh_done = sem("oh_done")
        node_done = sem("node_done")
        acc_done = sem("acc_done")
        fb_loaded = sem("fb_loaded")
        fb_step = sem("fb_step")
        fb_turn = sem("fb_turn")
        fb_oh = sem("fb_oh")
        fb_mm = sem("fb_mm")
        sums_ready = sem("sums_ready")
        nodes_turned = sem("nodes_turned")
        ln_step = sem("ln_step")
        var_ready = sem("var_ready")
        std_ready = sem("std_ready")
        y_ready = sem("y_ready")
        stored = sem("stored")

        block = ctx.enter_context(nc.Block())

        HEAD = 5
        TURNS = (NB - 2 - HEAD) // RING

        def steps(eng, step, lead):
            for c in range(HEAD):
                step(Block(0, c))
            with eng.Fori(0, TURNS) as turn:
                for c in range(HEAD, HEAD + RING):
                    step(Block(turn, c))
            for c in range(HEAD + RING * TURNS, NB + lead):
                step(Block(0, c))

        def directions(b, v):
            return geo_r[b.c % RING][:, :, 0:3].unsqueeze(3).to_broadcast([P, T, 3, v])

        @block.sync
        def _(sp):
            def load(b):
                n = b.c % RING
                if b.known >= RING:
                    sp.wait_ge(gathered[n], b.turns(T * 16))
                    sp.wait_ge(rows_final[n], b.turns(T * 16))
                at = b.times(BE)
                sp.dma_start(src_r[n][:], src[bass.ds(at, BE)].rearrange("(p t) -> p t", t=T)).then_inc(idx_loaded[n], 16)
                sp.dma_start(dst_r[n][:], dst[bass.ds(at, BE)].rearrange("(p t) -> p t", t=T)).then_inc(idx_loaded[n], 16)
                if b.known >= RING:
                    sp.wait_ge(embt_done, b.times(1, 1 - RING))
                sp.dma_start(emb_r[n][:], emb[bass.ds(at, BE), :].rearrange("(p t) k -> p (t k)", t=T)).then_inc(emb_loaded[n], 16)

            def load_geo(b):
                n = b.c % RING
                if b.known >= RING:
                    sp.wait_ge(eo_done, b.times(1, 1 - RING))
                    sp.wait_ge(far_done, b.times(1, 1 - RING))
                sp.dma_start(geo_r[n][:], geo_dram[bass.ds(b.times(BE), BE), :].rearrange("(p t) k -> p t k", t=T)).then_inc(geo_loaded[n], 16)

            def load_window(b):
                n = b.c % 2
                if b.known >= 2:
                    sp.wait_ge(far_t_done, b.times(1, -1))
                    sp.wait_ge(rows_done, b.times(1, -1))
                sp.dma_start(place_r[n][:], place_dram[bass.ds(b.times(BE), BE)].unsqueeze(0)
                             .to_broadcast([2 * WIN, BE])).then_inc(window_loaded[n], 16)
                base = sp.value_load(bases[0:1, bass.ds(b.times(1), 1)], min_val=0, max_val=N - 1)
                sp.dma_start(window_r[n][:, 0, :], x_dram[0:2, bass.ds(base, WIN), :]).then_inc(window_loaded[n], 16)
                sp.dma_start(window_r[n][0:WIN, 1, :], x_dram[2, bass.ds(base, WIN), :]).then_inc(window_loaded[n], 16)

            def keep(b):
                sp.wait_ge(eo_done, b.times(1, 1))
                sp.dma_start(eo_all[:, bass.ds(b.times(1), 1), :].rearrange("p b (t d) -> p (b t) d", t=T),
                             eo_r[b.c % 2][:, :, W:W + D]).then_inc(eo_kept[b.c % 2], 16)

            sp.dma_start(dst_b[:], dst.rearrange("(b e) -> b e", b=NB)).then_inc(dst_loaded, 16)
            sp.dma_start(xn[:], x.rearrange("(p m) d -> p m d", p=P)).then_inc(nodes_loaded, 16)
            sp.dma_start(vec_b, vec.rearrange("(b e) k -> b e k", b=NB)).then_inc(vec_loaded, 16)
            load(Block(0, 0))
            sp.wait_ge(zeroed, 2)
            sp.dma_start(x_dram[:, N:N + WIN, :].rearrange("n m d -> m n d"), no_rows[:]).then_inc(x_stored, 16)
            sp.dma_start(bases[:], dst.rearrange("(b e) -> e b", b=NB)[0:1, :],
                         allow_slow_non_contiguous=True).then_inc(bases_loaded, 16)
            sp.dma_start(wgt_b[:], weight.rearrange("(b e) -> b e", b=NB)).then_inc(weight_loaded, 16)
            for t in range(T):
                for n, w in enumerate((w11, w21)):
                    sp.dma_start(w1bd[10 * t:10 * t + 10, t, n, :], w).then_inc(w1_loaded, 16)
            sp.wait_ge(x_part_ready, 3)
            for n in range(3):
                sp.dma_start(x_dram[n, 0:N, :].rearrange("(p m) d -> p m d", p=P), x_part[:, n, :, :]).then_inc(x_stored, 16)
            sp.wait_ge(place_ready, 1)
            sp.dma_start(place_dram.rearrange("(b e) -> b e", b=NB), place_b[:]).then_inc(place_stored, 16)
            load(Block(0, 1))
            sp.wait_ge(bases_loaded, 16)
            sp.wait_ge(x_stored, 64)
            sp.wait_ge(place_stored, 16)
            load_window(Block(0, 0))
            load_window(Block(0, 1))
            for c in range(2, RING):
                load(Block(0, c))
            load_window(Block(0, 2))
            sp.wait_ge(geo_ready, 1)
            sp.dma_start(geo_dram.rearrange("(b e) k -> b e k", b=NB), geo_b).then_inc(geo_stored, 16)
            sp.wait_ge(geo_stored, 16)
            for c in range(2):
                load_geo(Block(0, c))
            load_window(Block(0, 3))
            for c in range(2, RING):
                load_geo(Block(0, c))
            load(Block(0, RING))
            load(Block(0, RING + 1))
            for c in range(4, 6):
                load_window(Block(0, c))

            def step(b):
                if (b + 6).real:
                    load(b + 6)
                    load_window(b + 6)
                if (b + RING).real:
                    load_geo(b + RING)
                if b.real:
                    keep(b)

            for c in range(3):
                step(Block(0, c))
            turns = (NB - 6 - 3) // RING
            with sp.Fori(0, turns) as turn:
                for c in range(3, 3 + RING):
                    step(Block(turn, c))
            for c in range(3 + RING * turns, NB):
                step(Block(0, c))

            sp.wait_ge(misfits_ready, 1)
            flag = sp.value_load(misfits[0:1, 0:1], min_val=0, max_val=2 * NB)
            with sp.If(flag):
                sp.dma_start(dst_all[:], dst.rearrange("(b p t) -> p b t", p=P, t=T)).then_inc(fb_loaded, 16)
            with sp.Else():
                sp.nop()
            sp.wait_ge(y_ready, 1)
            sp.dma_start(out.rearrange("(p m) d -> p m d", p=P), yn[:]).then_inc(stored, 16)
            sp.wait_ge(stored, 16)
            for n in range(2):
                sp.wait_ge(eo_kept[n], 16 * len(range(n, NB, 2)))

        @block.gpsimd
        def _(pool):
            nc.gpsimd.memset(w1bd[:].rearrange("r t n j -> r (t n j)"), 0.0).then_inc(zeroed, 1)
            nc.gpsimd.memset(no_rows[:], 0.0).then_inc(zeroed, 1)
            nc.gpsimd.memset(ones[:], 1.0).then_inc(pool_consts, 1)
            nc.gpsimd.iota(iota_i[:], pattern=[[1, P]], base=0, channel_multiplier=0).then_inc(pool_consts, 1)
            nc.gpsimd.iota(rank_i[:], pattern=[[0, 1]], base=0, channel_multiplier=1).then_inc(pool_consts, 1)
            nc.gpsimd.memset(ident[:], 0.0).then_inc(pool_consts, 1)
            pool.wait_ge(pool_consts, 4)
            nc.gpsimd.affine_select(out=ident[:], in_=ident[:], compare_op=ALU.not_equal, fill=1.0, base=0,
                                    pattern=[[-1, 128]], channel_multiplier=1).then_inc(pool_consts, 1)
            nc.gpsimd.memset(acc[:], 0.0).then_inc(zeroed, 1)

            def gathers(b, first, end):
                n = b.c % RING
                if first == 0:
                    pool.wait_ge(idx_loaded[n], b.turns(32, 32))
                    if b.known >= RING:
                        pool.wait_ge(f1_copied, b.times(5, 5 - 5 * RING))
                    pool.sem_inc(gather_turn, 1)
                for t in range(first, end):
                    nc.gpsimd.indirect_dma_start(
                        x_r[n][:, t, 0, :], None, x, bass.IndirectOffsetOnAxis(src_r[n][:, t:t + 1], axis=0)
                    ).then_inc(gathered[n], 16)

            def rows_at_destinations(b, general):
                n = b.c % RING
                if general:
                    pool.wait_ge(rows_copied, b.times(1, 1))
                    pool.sem_inc(gather_turn, 1)
                    for t in range(T):
                        nc.gpsimd.indirect_dma_start(
                            x_r[n][:, t, 1, :], None, x, bass.IndirectOffsetOnAxis(dst_r[n][:, t:t + 1], axis=0)
                        ).then_inc(rows_final[n], 16)
                else:
                    pool.sem_inc(rows_final[n], T * 16)

            def f1_make(b):
                n, f1 = b.c % RING, f1_r[b.c % 2]
                pool.wait_ge(geo_loaded[n], b.turns(16, 16))
                pool.wait_ge(f1_copied, b.times(5, 5))
                nc.gpsimd.tensor_tensor(f1_products[:], f1[:, :, 3:6, :], directions(b, V1), ALU.mult).then_inc(f1_step, 1)
                pool.wait_ge(f1_step, b.times(2, 1))
                nc.gpsimd.tensor_tensor(f1_pair[:], f1_products[:, :, 0, :], f1_products[:, :, 1, :], ALU.add).then_inc(f1_step, 1)
                pool.wait_ge(f1_step, b.times(2, 2))
                nc.gpsimd.tensor_tensor(f1[:, :, 0, :], f1_pair[:], f1_products[:, :, 2, :], ALU.add).then_inc(f1_made, 1)

            def h_rest(b, part):
                pool.wait_ge(part_ready[part], b.times(1, 1))
                slot = [n for n, (k, _) in enumerate(SLOTS) if k == part][0]
                h = h_r[b.c % 2][:]
                nc.gpsimd.tensor_tensor(h, h, hp_r[b.c % 2][:, :, :, slot, :].rearrange("p k t j -> p t k j"),
                                        ALU.subtract).then_inc(rest_ready, 1)

            def fold2(b):
                p2 = p2_r[b.c % 2]
                pool.wait_ge(p2_done, b.times(2 * NG, 2 * NG))
                vv, ss = (p2[:, :, k:k + 2].rearrange("p t k u w -> p t (k u w)") for k in (0, 2))
                nc.gpsimd.tensor_tensor(ss, ss, vv, ALU.add).then_inc(fold2_done, 1)

            def output(b):
                eo, geo = eo_r[b.c % 2], geo_r[b.c % RING]
                pool.wait_ge(tanh_done, b.times(1, 1))
                if b.known >= 2:
                    pool.wait_ge(node_done, b.times(1, -1))
                    pool.wait_ge(eo_kept[b.c % 2], b.pairs(16))
                nc.gpsimd.tensor_tensor(eo[:, :, 0:2 * W], th_r[b.c % 2][:].rearrange("p t k w -> p t (k w)"),
                                        geo[:, :, 4:5].to_broadcast([P, T, 2 * W]), ALU.mult).then_inc(out_step, 1)
                pool.wait_ge(out_step, b.times(1, 1))
                pool.wait_ge(vectors_step, b.times(2, 2))
                nc.gpsimd.tensor_tensor(eo[:, :, 2 * W:].rearrange("p t (u k) -> p t k u", k=3), vectors_r[b.c % 2][:],
                                        eo[:, :, 0:W].unsqueeze(2).to_broadcast([P, T, 3, W]), ALU.mult).then_inc(eo_done, 1)

            def run(general):
                def step(b):
                    if (b + -2).real:
                        fold2(b + -2)
                    if (b + 3).real:
                        gathers(b + 3, 0, 1)
                    if (b + 1).real:
                        h_rest(b + 1, 1)
                        f1_make(b + 1)
                    if (b + 3).real:
                        gathers(b + 3, 1, 3)
                    if (b + 2).real:
                        h_rest(b + 2, 0)
                    if (b + 3).real:
                        gathers(b + 3, 3, T)
                    if (b + 2).real:
                        rows_at_destinations(b + 2, general)
                    if (b + -2).real:
                        output(b + -2)

                step(Block(0, -2))
                step(Block(0, -1))
                steps(pool, step, 2)

            for n in range(2):
                of = xn if n == 0 else yn
                pool.wait_ge(x_part_ready, n + 1)
                nc.gpsimd.tensor_tensor(yn[:], of[:], x_part[:, n, :, :], ALU.subtract).then_inc(x_rest, 1)
            gathers(Block(0, 0), 0, T)
            pool.wait_ge(misfits_ready, 1)
            flag = pool.value_load(misfits[0:1, 0:1], min_val=0, max_val=2 * NB)
            with pool.If(flag):
                run(True)
            with pool.Else():
                run(False)

        @block.scalar
        def _(act):
            def slots(w):
                return w.unsqueeze(0).to_broadcast([S, J, w.shape[1]])

            w2_columns = [(w12, to, of, cols) for to, of, cols in ((0, 128, 128), (128, 0, 128), (256, 256, 256))]
            w2_columns += [(w22, C1 + to, of, cols) for to, of, cols in
                           ((0, 192, 64), (64, 64, 64), (128, 128, 64), (192, 0, 64), (256, 256, 128))]
            for n in range(3):
                for w, to, of, cols in w2_columns[3 * n:3 * n + 3]:
                    act.dma_start(w2f[:, to:to + cols], slots(w[:, of:of + cols])).then_inc(w2_loaded, 16)
                if n == 0:
                    act.wait_ge(nodes_loaded, 16)
                else:
                    act.wait_ge(x_rest, n)
                nc.scalar.copy(x_part[:, n, :, :], xn[:] if n == 0 else yn[:]).then_inc(x_part_ready, 1)
            act.wait_ge(setup_step, 7 + 3)
            nc.scalar.activation(nrm_b[:], n2_b[:], ACT.Sqrt).then_inc(norm_ready, 1)
            act.wait_ge(place_ready, 1)
            nc.scalar.copy(geo_b[:, :, 3], place_b[:]).then_inc(geo_copied, 1)
            act.wait_ge(weight_loaded, 16)
            nc.scalar.copy(geo_b[:, :, 4], wgt_b[:]).then_inc(geo_copied, 1)
            def f1_copies(b):
                n, f1 = b.c % RING, f1_r[b.c % 2]
                act.wait_ge(gathered[n], b.turns(T * 16, T * 16))
                act.wait_ge(rows_final[n], b.turns(T * 16, T * 16))
                if b.known >= 2:
                    act.wait_ge(p1_done, b.times(2 * NG, -2 * NG))
                xs = x_r[n][:]
                for k, of in ((1, xs[:, :, :, 0:8]), (2, xs[:, :, :, 0:8])) + tuple(
                        (3 + k, xs[:, :, :, 8 + k:D:3]) for k in range(3)):
                    nc.scalar.copy(f1[:, :, k, :].rearrange("p t (h u) -> p t h u", h=2), of).then_inc(f1_copied, 1)

            def one_hot(b):
                n = b.c % RING
                act.wait_ge(geo_loaded[n], b.turns(16, 16))
                if b.known >= 1:
                    act.wait_ge(oh_done, b.times(1))
                for t in range(T):
                    last = nc.scalar.activation(far[:, t, :], iota[:, 0:WIN], ACT.Abs, bias=geo_r[n][:, t, 3:4])
                last.then_inc(far_done, 1)
                act.wait_ge(far_done, b.times(1, 1))
                if b.known >= 2:
                    act.wait_ge(node_done, b.times(1, -1))
                nc.scalar.activation(oh_r[b.c % 2][:], far[:], ACT.Relu, scale=-1.0, bias=ones[0:P, :]).then_inc(oh_done, 1)

            def f2_copies(b):
                if b.known >= 2:
                    act.wait_ge(p2_done, b.times(2 * NG, -2 * NG))
                act.wait_ge(sum1_done, b.times(1, 1))
                nc.scalar.copy(f2_r[b.c % 2][:, :, 2:5, :],
                               sum1[:, :, 0:1, :].to_broadcast([P, T, 3, W])).then_inc(f2_copied, 1)

            def f2_second(b):
                act.wait_ge(f2_step, b.times(4, 4))
                nc.scalar.copy(f2_r[b.c % 2][:, :, 1, :], f2_r[b.c % 2][:, :, 0, :]).then_inc(f2_twice, 1)

            def tanhs(b):
                if b.known >= 2:
                    act.wait_ge(eo_done, b.times(1, -1))
                act.wait_ge(sum2_done, b.times(1, 1))
                nc.scalar.activation(th_r[b.c % 2][:], sum2[:, :, 0:2, :], ACT.Tanh).then_inc(tanh_done, 1)

            def hidden(b):
                act.wait_ge(h_done, b.times(1, 1))
                if b.known >= 2:
                    act.wait_ge(part_ready[2], b.times(1, -1))
                nc.scalar.activation(h_r[b.c % 2][:].rearrange("p t n j -> p (t n j)"), h_ps, ACT.Relu,
                                     scale=1.0 / math.sqrt(10.0)).then_inc(h_ready, 1)

            def h_part(b, part):
                slots = [n for n, (k, _) in enumerate(SLOTS) if k == part]
                if part == 0:
                    act.wait_ge(h_ready, b.times(1, 1))
                    if b.known >= 2:
                        act.wait_ge(ht_done[1], b.times(1, -1))
                else:
                    act.wait_ge(rest_ready, b.times(2, part))
                hp, h = hp_r[b.c % 2], h_r[b.c % 2]
                for k in range(2):
                    last = nc.scalar.copy(hp[:, k, :, slots[0]:slots[-1] + 1, :],
                                          h[:, :, k, :].unsqueeze(2).to_broadcast([P, T, len(slots), J]))
                last.then_inc(part_ready[part], 1)

            def ht_copy(b, k):
                if b.known >= 2:
                    act.wait_ge((w1_done, w2_done)[k], b.times(NG, -NG))
                act.wait_ge(ht_done[k], b.times(1, 1))
                nc.scalar.copy(ht_r[k][b.c % 2][:].rearrange("r (t e) -> r t e", t=T), ht_ps).then_inc(ht_copied[k], 1)

            def embt_copy(b):
                if b.known >= 2:
                    act.wait_ge(h_done, b.times(1, -1))
                act.wait_ge(rows_done, b.times(1, 1))
                nc.scalar.copy(embt_r[b.c % 2][:], embt_ps).then_inc(embt_copied, 1)

            def destination_hot(b):
                n = b.c % 2
                act.wait_ge(window_loaded[n], b.pairs(48, 48))
                if b.known >= 1:
                    act.wait_ge(oht_done, b.times(1))
                nc.scalar.activation(far_t[:], place_r[n][:].rearrange("m (p t) -> m t p", t=T), ACT.Abs,
                                     bias=rank[:]).then_inc(far_t_done, 1)
                act.wait_ge(far_t_done, b.times(1, 1))
                if b.known >= 2:
                    act.wait_ge(rows_done, b.times(1, -1))
                nc.scalar.activation(oht_r[n][:], far_t[:], ACT.Relu, scale=-1.0, bias=ones[:]).then_inc(oht_done, 1)

            def rows_copy(b):
                act.wait_ge(rows_done, b.times(1, 1))
                nc.scalar.copy(x_r[b.c % RING][:, :, 1, :], rows_ps).then_inc(rows_copied, 1)

            def step(b):
                if (b + -1).real:
                    f2_copies(b + -1)
                if (b + 2).real:
                    embt_copy(b + 2)
                    rows_copy(b + 2)
                if (b + 1).real:
                    f1_copies(b + 1)
                    h_part(b + 1, 2)
                if (b + 2).real:
                    hidden(b + 2)
                    h_part(b + 2, 0)
                if (b + -1).real:
                    f2_second(b + -1)
                if (b + 1).real:
                    ht_copy(b + 1, 0)
                if (b + -2).real:
                    tanhs(b + -2)
                    one_hot(b + -2)
                if (b + 3).real:
                    destination_hot(b + 3)
                if (b + 1).real:
                    ht_copy(b + 1, 1)
                if (b + 2).real:
                    h_part(b + 2, 1)

            act.wait_ge(w2_loaded, 16 * 8)
            c1, c2 = 0.25 / math.sqrt(32.0), 1.0 / 16.0
            for a, b, c in ((0, 256, c1), (256, 384, c1 * SQRT3), (384, C1, c1),
                            (C1, C1 + 256, c2), (C1 + 256, C1 + 320, c2 * SQRT3), (C1 + 320, C1 + C2, c2)):
                nc.scalar.mul(w2f[:, a:b], w2f[:, a:b], c).then_inc(w2_scaled, 1)
            act.wait_ge(w2_scaled, 6)
            nc.scalar.copy(w2part[0][:], w2f[:]).then_inc(w2_part, 1)
            act.wait_ge(iota_ready, 2)
            destination_hot(Block(0, 0))
            step(Block(0, -2))
            for n in (1, 2):
                act.wait_ge(w2_rest, n)
                nc.scalar.copy(w2part[n][:], w2f[:]).then_inc(w2_part, 1)
            step(Block(0, -1))
            steps(act, step, 3)
            act.wait_ge(var_ready, 1)
            nc.scalar.activation(st[:, 2, :], st[:, 1, :], ACT.Sqrt).then_inc(std_ready, 1)

        @block.vector
        def _(dve):
            setup = [0]

            def link(ins):
                setup[0] += 1
                ins.then_inc(setup_step, 1)
                dve.wait_ge(setup_step, setup[0])

            dve.wait_ge(pool_consts, 5)
            nc.vector.tensor_copy(ident_h[:], ident[0:P, 0:P]).then_inc(ident_ready, 1)
            nc.vector.tensor_copy(iota[:], iota_i[:]).then_inc(iota_ready, 1)
            rows = ident[0:S * J, 0:S * J].rearrange("p (s j) -> p s j", s=S)
            for n, (a, b, c) in enumerate(((0, 4, 3), (1, 5, 3), (2, 3, 1), (5, 6, 1))):
                link(nc.vector.tensor_reduce(slot_mask[:, n:n + 1], rows[:, a:b:c, :], AX.XY, ALU.add))
            link(nc.vector.tensor_tensor(slot_mask[:, 0:1], slot_mask[:, 0:1], slot_mask[:, 3:4], ALU.add))
            link(nc.vector.tensor_copy(rank[:], rank_i[:]))
            link(nc.vector.tensor_scalar(rank_high[:], rank[:], float(WIN), float(WIN), ALU.is_ge, ALU.mult))
            nc.vector.tensor_tensor(rank[:], rank[:], rank_high[:], ALU.subtract).then_inc(iota_ready, 1)
            dve.wait_ge(dst_loaded, 16)
            link(nc.vector.tensor_copy(dstf_b[:], dst_b[:]))
            nc.vector.tensor_scalar(place_b[:], dstf_b[:], -1.0, dstf_b[:, 0:1], ALU.mult, ALU.add).then_inc(place_ready, 1)
            dve.wait_ge(vec_loaded, 16)
            link(nc.vector.tensor_tensor(geo_b[:, :, 0:3], vec_b, vec_b, ALU.mult))
            link(nc.vector.tensor_reduce(n2_b[:], geo_b[:, :, 0:3], AX.X, ALU.add))
            dve.wait_ge(place_ready, 1)
            link(nc.vector.tensor_reduce(ext[:, 0:1], place_b[:], AX.X, ALU.max))
            link(nc.vector.tensor_reduce(ext[:, 1:2], place_b[:], AX.X, ALU.min))
            link(nc.vector.tensor_scalar(ext[:, 0:1], ext[:, 0:1], 0.0, None, ALU.is_gt))
            link(nc.vector.tensor_scalar(ext[:, 1:2], ext[:, 1:2], 1.0 - WIN, None, ALU.is_lt))
            nc.vector.tensor_tensor(ext[:, 2:3], ext[:, 0:1], ext[:, 1:2], ALU.add).then_inc(misfit_parts, 1)
            dve.wait_ge(misfit_sum, 1)
            nc.vector.tensor_copy(misfits[:], ps[0:1, 5, 0:1]).then_inc(misfits_ready, 1)
            dve.wait_ge(norm_ready, 1)
            link(nc.vector.reciprocal(inv_b[:], nrm_b[:]))
            link(nc.vector.tensor_tensor(dstf_b[:], n2_b[:], inv_b[:], ALU.mult))
            link(nc.vector.tensor_tensor(dstf_b[:], dstf_b[:], inv_b[:], ALU.mult))
            link(nc.vector.tensor_scalar(dstf_b[:], dstf_b[:], -0.5, 1.5, ALU.mult, ALU.add))
            link(nc.vector.tensor_tensor(inv_b[:], inv_b[:], dstf_b[:], ALU.mult))
            dve.wait_ge(geo_copied, 2)
            nc.vector.tensor_tensor(geo_b[:, :, 0:3], vec_b, inv_b[:].unsqueeze(2).to_broadcast([NB, BE, 3]),
                                    ALU.mult).then_inc(geo_ready, 1)
            for n in range(2):
                dve.wait_ge(w2_part, n + 1)
                nc.vector.tensor_tensor(w2f[:], w2f[:], w2part[n][:], ALU.subtract).then_inc(w2_rest, 1)
            link(nc.vector.tensor_scalar(w2s[:], w2part[0][:], slot_mask[:, 0:1], None, ALU.mult))
            dve.wait_ge(w2_part, 3)
            for n in (1, 2):
                last = nc.vector.scalar_tensor_tensor(out=w2s[:], in0=w2part[n][:], scalar=slot_mask[:, n:n + 1],
                                                      in1=w2s[:], op0=ALU.mult, op1=ALU.add)
                if n == 1:
                    link(last)
            last.then_inc(w2_ready, 1)

            def f2_make(b, part):
                f2, dirs = f2_r[b.c % 2], directions(b, W)
                if part == 0:
                    dve.wait_ge(f2_copied, b.times(1, 1))
                    nc.vector.tensor_tensor(sv_directed[:], sum1[:, :, 1:2, :].to_broadcast([P, T, 3, W]), dirs,
                                            ALU.mult).then_inc(f2_step, 1)
                elif part == 1:
                    dve.wait_ge(f2_step, b.times(4, 1))
                    nc.vector.tensor_tensor(f2[:, :, 5:8, :], sv_directed[:], sum1[:, :, 2:5, :], ALU.add).then_inc(f2_step, 1)
                elif part == 2:
                    dve.wait_ge(f2_step, b.times(4, 2))
                    nc.vector.tensor_tensor(f2_products[:], f2[:, :, 5:8, :], dirs, ALU.mult).then_inc(f2_step, 1)
                else:
                    dve.wait_ge(f2_step, b.times(4, 3))
                    nc.vector.tensor_reduce(f2[:, :, 0, :], f2_products[:].rearrange("p t k u -> p t u k"), AX.X,
                                            ALU.add).then_inc(f2_step, 1)

            def times(wps, f, p):
                _, t, k, u, w = p.shape
                k_w = wps.shape[2]
                if k_w == k:
                    return nc.vector.tensor_tensor(p.rearrange("p t k u w -> p t (k u) w"),
                                                   wps.rearrange("p t k (u w) -> p t (k u) w", w=w),
                                                   f.rearrange("p t k u -> p t (k u)").unsqueeze(3).to_broadcast([P, t, k * u, w]),
                                                   ALU.mult)
                return nc.vector.tensor_tensor(p, wps.rearrange("p t k (u w) -> p t k u w", w=w).to_broadcast([P, t, k, u, w]),
                                               f.unsqueeze(4).to_broadcast([P, t, k, u, w]), ALU.mult)

            def products1(b, first, end):
                f1, p1 = f1_r[b.c % 2], p1_r[b.c % 2]
                dve.wait_ge(f1_made, b.times(1, 1))
                if b.known >= 2 and first == 0:
                    dve.wait_ge(sum1_done, b.times(1, -1))
                for n in range(first, end):
                    t, tiles, bank = GROUPS[0][n]
                    wps = ps[0:P, bank:bank + tiles, :].rearrange("p t (g v) -> p t g v", g=4)
                    dve.wait_ge(w1_done, b.times(NG, n + 1))
                    times(wps[:, :, 0:3], f1[:, t:t + tiles, 0:3], p1[:, t:t + tiles, 0:3]).then_inc(p1_done, 1)
                    times(wps[:, :, 3:4], f1[:, t:t + tiles, 3:6], p1[:, t:t + tiles, 3:6]).then_inc(p1_done, 1)

            def fold1(b):
                p1 = p1_r[b.c % 2]
                dve.wait_ge(p1_done, b.times(2 * NG, 2 * NG))
                vv, ss = (p1[:, :, k].rearrange("p t u w -> p t (u w)") for k in (0, 1))
                nc.vector.tensor_tensor(ss, ss, vv, ALU.add).then_inc(fold1_done, 1)

            def halve1(b):
                p1 = p1_r[b.c % 2]
                dve.wait_ge(fold1_done, b.times(1, 1))
                lo, hi = (p1[:, :, 1:K1, a:a + HALF1, :].rearrange("p t k u w -> p t k (u w)") for a in (0, V1 - HALF1))
                nc.vector.tensor_tensor(lo, lo, hi, ALU.add).then_inc(half1_done, 1)

            def products2(b, first, end):
                f2, p2 = f2_r[b.c % 2], p2_r[b.c % 2]
                if first == 0:
                    dve.wait_ge(f2_twice, b.times(1, 1))
                    if b.known >= 2:
                        dve.wait_ge(sum2_done, b.times(1, -1))
                for n in range(first, end):
                    t, tiles, bank = GROUPS[1][n]
                    wps = ps[0:P, bank:bank + tiles, 0:C2].rearrange("p t (g v) -> p t g v", g=6)
                    dve.wait_ge(w2_done, b.times(NG, n + 1))
                    times(wps[:, :, 0:5], f2[:, t:t + tiles, 0:5], p2[:, t:t + tiles, 0:5]).then_inc(p2_done, 1)
                    times(wps[:, :, 5:6], f2[:, t:t + tiles, 5:8], p2[:, t:t + tiles, 5:8]).then_inc(p2_done, 1)

            def vectors(b, part):
                vec2 = vectors_r[b.c % 2]
                if part == 0:
                    dve.wait_ge(tanh_done, b.times(1, 1))
                    if b.known >= 2:
                        dve.wait_ge(eo_done, b.times(1, -1))
                    nc.vector.tensor_tensor(vec2[:], sum2[:, :, 2:3, :].to_broadcast([P, T, 3, W]), directions(b, W),
                                            ALU.mult).then_inc(vectors_step, 1)
                else:
                    dve.wait_ge(vectors_step, b.times(2, 1))
                    nc.vector.tensor_tensor(vec2[:], vec2[:], sum2[:, :, 3:6, :], ALU.add).then_inc(vectors_step, 1)

            def accumulate(b):
                base = dve.value_load(bases[0:1, bass.ds(b.times(1), 1)], min_val=0, max_val=N - 1)
                dve.wait_ge(node_done, b.times(1, 1))
                if b.known >= 1:
                    dve.wait_ge(acc_done, b.times(1))
                nodes = acc[:, bass.ds(base, WIN)]
                nc.vector.tensor_tensor(nodes, nodes, node_ps, ALU.add).then_inc(acc_done, 1)

            def step(b):
                if b.real:
                    products1(b, 0, NG)
                if (b + -1).real:
                    f2_make(b + -1, 0)
                if (b + -3).real:
                    accumulate(b + -3)
                if (b + -1).real:
                    f2_make(b + -1, 1)
                if b.real:
                    fold1(b)
                if (b + -1).real:
                    f2_make(b + -1, 2)
                if (b + -1).real:
                    f2_make(b + -1, 3)
                if b.real:
                    halve1(b)
                if (b + -1).real:
                    products2(b + -1, 0, 1)
                if (b + -2).real:
                    vectors(b + -2, 0)
                if (b + -1).real:
                    products2(b + -1, 1, 2)
                if (b + -2).real:
                    vectors(b + -2, 1)
                if (b + -1).real:
                    products2(b + -1, 2, NG)

            step(Block(0, -2))
            step(Block(0, -1))
            dve.wait_ge(bases_loaded, 16)
            dve.wait_ge(zeroed, 3)
            steps(dve, step, 3)

            flag = dve.value_load(misfits[0:1, 0:1], min_val=0, max_val=2 * NB)
            with dve.If(flag):
                dve.wait_ge(fb_loaded, 16)
                dve.wait_ge(acc_done, NB)
                nc.vector.memset(acc[:], 0.0).then_inc(fb_step, 1)
                dve.wait_ge(fb_step, 1)
                with dve.Fori(0, NB) as i:
                    nc.vector.tensor_copy(dst_w[:], dst_all[:, bass.ds(i, 1), :].rearrange("p b t -> p (b t)")).then_inc(fb_step, 1)
                    nc.vector.tensor_copy(eo_s[:].rearrange("p t d -> p (t d)"),
                                          eo_all[:, bass.ds(i, 1), :].rearrange("p b n -> p (b n)")).then_inc(fb_step, 1)
                    dve.wait_ge(fb_step, i * (2 + 2 * NT) + 3)
                    dve.sem_inc(fb_turn, 1)
                    with dve.Fori(0, NT) as m:
                        nc.vector.tensor_tensor(oh_w[:], iota[:].unsqueeze(1).to_broadcast([P, T, P]),
                                                dst_w[:].unsqueeze(2).to_broadcast([P, T, P]), ALU.is_equal).then_inc(fb_oh, 1)
                        dve.wait_ge(fb_oh, i * NT + m + 1)
                        nc.vector.tensor_scalar(dst_w[:], dst_w[:], -float(P), None, ALU.add).then_inc(fb_step, 1)
                        dve.wait_ge(fb_mm, i * NT + m + 1)
                        nodes = acc[:, bass.ds(m * P, P)]
                        nc.vector.tensor_tensor(nodes, nodes, ps[0:D, 0, 0:P], ALU.add).then_inc(fb_step, 1)
                        dve.wait_ge(fb_step, i * (2 + 2 * NT) + m * 2 + 5)
                nc.vector.engine_nop().then_inc(sums_ready, 1)
            with dve.Else():
                dve.wait_ge(acc_done, NB)
                nc.vector.engine_nop().then_inc(sums_ready, 1)

            turned = [0]

            def chain(ins):
                turned[0] += 1
                ins.then_inc(ln_step, 1)
                dve.wait_ge(ln_step, turned[0])

            def wide(a):
                return a.unsqueeze(2).to_broadcast([P, NT, D])

            dve.wait_ge(nodes_loaded, 16)
            dve.wait_ge(nodes_turned, 1)
            chain(nc.vector.tensor_tensor(yn[:].rearrange("p m d -> p (m d)"), xn[:].rearrange("p m d -> p (m d)"),
                                          ps[0:P].rearrange("p b c -> p (b c)")[:, 0:NT * D], ALU.add))
            chain(nc.vector.tensor_reduce(st[:, 0, :], yn[:], AX.X, ALU.add))
            chain(nc.vector.tensor_scalar(st[:, 0, :], st[:, 0, :], 1.0 / D, None, ALU.mult))
            chain(nc.vector.tensor_tensor(yn[:], yn[:], wide(st[:, 0, :]), ALU.subtract))
            chain(nc.vector.tensor_tensor(xn[:], yn[:], yn[:], ALU.mult))
            chain(nc.vector.tensor_reduce(st[:, 5, :], xn[:], AX.X, ALU.add))
            nc.vector.tensor_scalar(st[:, 1, :], st[:, 5, :], 1.0 / D, EPS, ALU.mult, ALU.add).then_inc(var_ready, 1)
            dve.wait_ge(std_ready, 1)
            chain(nc.vector.reciprocal(st[:, 3, :], st[:, 2, :]))
            chain(nc.vector.tensor_tensor(st[:, 4, :], st[:, 3, :], st[:, 1, :], ALU.mult))
            chain(nc.vector.tensor_tensor(st[:, 4, :], st[:, 4, :], st[:, 3, :], ALU.mult))
            chain(nc.vector.tensor_scalar(st[:, 4, :], st[:, 4, :], -0.5, 1.5, ALU.mult, ALU.add))
            chain(nc.vector.tensor_tensor(st[:, 3, :], st[:, 3, :], st[:, 4, :], ALU.mult))
            nc.vector.tensor_tensor(yn[:], yn[:], wide(st[:, 3, :]), ALU.mult).then_inc(y_ready, 1)

        @block.tensor
        def _(pe):
            idn = ident[0:P, 0:P]
            pe.wait_ge(pool_consts, 5)

            def ht(b, k):
                pe.wait_ge(part_ready[2], b.times(1, 1))
                if k == 1:
                    pe.wait_ge(ht_copied[0], b.times(1, 1))
                elif b.known >= 1:
                    pe.wait_ge(ht_copied[1], b.times(1))
                if k == 0 and b.known >= 4:
                    pe.wait_ge(acc_done, b.times(1, -3))
                for t in range(T):
                    last = nc.tensor.transpose(ht_ps[:, t, :],
                                               hp_r[b.c % 2][:, k, t].rearrange("p s j -> p (s j)"), ident_h[:])
                last.then_inc(ht_done[k], 1)

            def w(b, k, n):
                if n == 0:
                    pe.wait_ge(ht_copied[k], b.times(1, 1))
                    if k == 0 and b.known == 0:
                        pe.wait_ge(w2_ready, 1)
                if k == 0 and n < 2 and b.known == 1:
                    pe.wait_ge(p1_done, 2 * NG)
                if n == 2:
                    pe.wait_ge((p1_done, p2_done)[k], b.times(2 * NG, 2))
                elif k == 0 and b.known >= 2:
                    pe.wait_ge(p2_done, b.times(2 * NG, 2 * (n + 2 - 2 * NG)))
                elif k == 1 and n == 0:
                    pe.wait_ge(p1_done, min_block(b + 1, 2 * NG, 4))
                elif k == 1:
                    pe.wait_ge(p1_done, min_block(b + 1, 2 * NG, 6))
                t, tiles, bank = GROUPS[k][n]
                cols = slice(0, C1) if k == 0 else slice(C1, C1 + C2)
                for i in range(tiles):
                    last = nc.tensor.matmul(ps[0:P, bank + i, 0:cols.stop - cols.start],
                                            ht_r[k][b.c % 2][:, P * (t + i):P * (t + i) + P], w2s[:, cols],
                                            start=True, stop=True)
                last.then_inc((w1_done, w2_done)[k], 1)

            def min_block(b, k, plus):
                return k * NB if isinstance(b.turn, int) and b.c >= NB else b.times(k, plus)

            def sums(u, left, p, dest):
                return nc.tensor.matmul(dest, idn, p[:, :, :, u, :], start=(u == 0), stop=(u == left - 1))

            def sum_1(b, u):
                left = V1 - HALF1
                if u == 0:
                    pe.wait_ge(half1_done, b.times(1, 1))
                    if b.known >= 1:
                        pe.wait_ge(f2_step, b.times(4, -2))
                last = sums(u, left, p1_r[b.c % 2][:, :, 1:K1], sum1)
                if u == left - 1:
                    last.then_inc(sum1_done, 1)

            def sum_2(b, u):
                if u == 0:
                    pe.wait_ge(fold2_done, b.times(1, 1))
                    if b.known == 0:
                        pe.wait_ge(misfits_ready, 1)
                    if b.known >= 1:
                        pe.wait_ge(vectors_step, b.times(2))
                last = sums(u, V2, p2_r[b.c % 2][:, :, 2:K2], sum2)
                if u == V2 - 1:
                    last.then_inc(sum2_done, 1)

            def over_nodes(b):
                pe.wait_ge(oh_done, b.times(1, 1))
                pe.wait_ge(ht_copied[1], min_block(b + 3, 1, 1))
                pe.wait_ge(eo_done, b.times(1, 1))
                for t in range(T):
                    last = nc.tensor.matmul(node_ps, eo_r[b.c % 2][:, t, W:W + D], oh_r[b.c % 2][:, t, :],
                                            start=(t == 0), stop=(t == T - 1))
                last.then_inc(node_done, 1)

            def embt(b):
                n = b.c % RING
                pe.wait_ge(emb_loaded[n], b.turns(16, 16))
                if b.known >= 1:
                    pe.wait_ge(h_ready, b.times(1))
                nc.tensor.matmul(embt_ps, emb_r[n][:], idn, start=True, stop=True).then_inc(embt_done, 1)

            def rows(b):
                pe.wait_ge(window_loaded[b.c % 2], b.pairs(48, 48))
                pe.wait_ge(oht_done, b.times(1, 1))
                for t in range(T):
                    nc.tensor.matmul(rows_ps[:, t, :], oht_r[b.c % 2][:, t, :], window_r[b.c % 2][:, 0, :],
                                     start=True, stop=False)
                    last = nc.tensor.matmul(rows_ps[:, t, :], oht_r[b.c % 2][0:WIN, t, :],
                                            window_r[b.c % 2][0:WIN, 1, :], start=False, stop=True)
                last.then_inc(rows_done, 1)

            def first_layer(b):
                pe.wait_ge(embt_copied, b.times(1, 1))
                pe.wait_ge(rows_copied, b.times(1, 1))
                if b.known == 0:
                    pe.wait_ge(w1_loaded, 16 * 2 * T)
                nc.tensor.matmul(h_ps, embt_r[b.c % 2][:], w1bd[:].rearrange("r t n j -> r (t n j)"),
                                 start=True, stop=True).then_inc(h_done, 1)

            def step(b):
                def part(which, lo, hi):
                    if which == 1 and b.real:
                        for u in range(lo, hi):
                            sum_1(b, u)
                    if which == 2 and (b + -2).real:
                        for u in range(lo, hi):
                            sum_2(b + -2, u)

                if (b + 2).real:
                    embt(b + 2)
                    rows(b + 2)
                if b.real:
                    w(b, 0, 2)
                if (b + -3).real:
                    over_nodes(b + -3)
                part(2, 0, 4)
                if (b + 2).real:
                    first_layer(b + 2)
                if (b + -1).real:
                    w(b + -1, 1, 0)
                part(2, 4, 6)
                if (b + 1).real:
                    ht(b + 1, 0)
                part(2, 6, 8)
                if (b + -1).real:
                    w(b + -1, 1, 1)
                part(1, 0, 0)
                if (b + 1).real:
                    ht(b + 1, 1)
                part(1, 0, 2)
                if (b + -1).real:
                    w(b + -1, 1, 2)
                part(1, 2, 5)
                if (b + 1).real:
                    w(b + 1, 0, 0)
                part(1, 5, 8)
                if (b + 1).real:
                    w(b + 1, 0, 1)
                part(1, 8, V1 - HALF1)

            pe.wait_ge(misfit_parts, 1)
            nc.tensor.matmul(ps[0:1, 5, 0:1], ext[:, 2:3], ones[0:NB, :], start=True, stop=True).then_inc(misfit_sum, 1)
            step(Block(0, -2))
            pe.wait_ge(ident_ready, 1)
            step(Block(0, -1))
            steps(pe, step, 3)

            flag = pe.value_load(misfits[0:1, 0:1], min_val=0, max_val=2 * NB)
            with pe.If(flag):
                with pe.Fori(0, NB) as i:
                    with pe.Fori(0, NT) as m:
                        pe.wait_ge(fb_oh, i * NT + m + 1)
                        for t in range(T):
                            last = nc.tensor.matmul(ps[0:D, 0, 0:P], eo_s[:, t, :], oh_w[:, t, :],
                                                    start=(t == 0), stop=(t == T - 1))
                        last.then_inc(fb_mm, 1)
            with pe.Else():
                pe.nop()
            pe.wait_ge(sums_ready, 1)
            for m in range(NT):
                b, at = divmod(m * D, 512)
                last = nc.tensor.transpose(ps[0:P, b, at:at + D], acc[:, m:N:NT], ident[0:D, 0:D])
            last.then_inc(nodes_turned, 1)


def kernel(x, src, dst, edge_attr_10, edge_attr_3, edge_weight,
           L0_gnn_fc1_w1, L0_gnn_fc1_w2, L0_gnn_fc2_w1, L0_gnn_fc2_w2):
    import numpy as np
    import concourse.bacc as bacc
    from concourse.bass_utils import run_bass_kernel_spmd

    nc = bacc.Bacc("TRN2", target_bir_lowering=False, num_devices=1)
    given = {"x": x, "src": src, "dst": dst, "emb": edge_attr_10, "vec": edge_attr_3, "weight": edge_weight,
             "w11": L0_gnn_fc1_w1, "w12": L0_gnn_fc1_w2, "w21": L0_gnn_fc2_w1, "w22": L0_gnn_fc2_w2}
    arrays, args = {}, {}
    for name, a in given.items():
        a = np.ascontiguousarray(a)
        arrays[f"in_{name}"] = a
        args[name] = nc.dram_tensor(f"in_{name}", a.shape, mybir.dt.from_np(a.dtype), kind="ExternalInput").ap()
    args["out"] = nc.dram_tensor("out_y", (N, D), F32, kind="ExternalOutput").ap()
    program(nc, **args)
    r = run_bass_kernel_spmd(nc, [arrays], core_ids=[0])
    return r.results[0]["out_y"]
```
